# Optimizing a Trainium2 kernel written in Bass

```python
import numpy as np
import jax
import jax.numpy as jnp

def _softmax(x, axis=-1):
    return jax.nn.softmax(x, axis=axis)

def _gelu(x):
    return jax.nn.gelu(x, approximate=True)

def _silu(x):
    return jax.nn.silu(x)

def _sigmoid(x):
    return jax.nn.sigmoid(x)

def _layernorm(x, axis=-1, eps=1e-05):
    m = jnp.mean(x, axis=axis, keepdims=True)
    v = jnp.var(x, axis=axis, keepdims=True)
    return (x - m) / jnp.sqrt(v + eps)

def _scatter_add(tgt, idx, src, axis=0):
    return tgt.at[idx].add(src)

def _segment_sum(src, seg, n):
    return jax.ops.segment_sum(src, seg, n)
kernel_name = 'mk_seq_postln_d1_jaxref_r8_e239b9'

def setup_inputs(seed: int=0):
    np.random.seed(seed)
    _w = jnp.asarray

    def _L0_attn_setup():
        import jax, jax.numpy as jnp
        import numpy as np
        import math
        B, T, C = (2, 256, 128)
        NH = 16
        HD = C // NH

        def _rope_factor(T, d, dtype):
            theta = 1.0 / 10000.0 ** (2.0 * jnp.arange(0, d // 2, dtype=jnp.float32) / d)
            seq = jnp.arange(1, T + 1, dtype=jnp.float32)
            ang = jnp.einsum('n,d->nd', seq, theta)
            ang = jnp.concatenate([ang, ang], axis=-1)
            return (jnp.cos(ang) + jnp.sin(ang)).astype(dtype)
        key = jax.random.key(seed)
        ks = jax.random.split(key, 5)
        s = 0.02
        return {'x': jax.random.normal(ks[0], (B, T, C), dtype=jnp.float32), 'W_attn': jax.random.normal(ks[1], (3 * C, C), dtype=jnp.float32) * s, 'b_attn': jax.random.normal(ks[2], (3 * C,), dtype=jnp.float32) * s, 'W_proj': jax.random.normal(ks[3], (C, C), dtype=jnp.float32) * s, 'b_proj': jax.random.normal(ks[4], (C,), dtype=jnp.float32) * s}
    _L0_attn_in = _L0_attn_setup()

    def _L0_ffn_setup():
        import jax, jax.numpy as jnp
        import numpy as np
        TOP_K = 2

        def _moe(x, Wr, br, W1, b1, W2, b2):
            B, S, D = x.shape
            E = Wr.shape[1]
            xt = x.reshape(-1, D)
            logits = xt @ Wr + br
            top_vals, top_idx = jax.lax.top_k(logits, TOP_K)
            mask = jnp.zeros_like(logits, dtype=bool).at[jnp.arange(xt.shape[0])[:, None], top_idx].set(True)
            sparse_logits = jnp.where(mask, logits, -jnp.inf)
            gate = jax.nn.softmax(sparse_logits, axis=-1)
            h = jax.nn.relu(jnp.einsum('td,edh->teh', xt, W1) + b1)
            y = jnp.einsum('teh,ehd->ted', h, W2) + b2
            out = jnp.einsum('ted,te->td', y, gate)
            return out.reshape(B, S, D)
        key = jax.random.key(seed)
        ks = jax.random.split(key, 5)
        B, S, D, E, H = (2, 256, 128, 8, 512)
        scale = 1.0 / np.sqrt(D)
        return {'x': jax.random.normal(ks[0], (B, S, D), dtype=jnp.float32), 'Wr': jax.random.normal(ks[1], (D, E), dtype=jnp.float32) * scale, 'br': jnp.zeros((E,), dtype=jnp.float32), 'W1': jax.random.normal(ks[2], (E, D, H), dtype=jnp.float32) * scale, 'b1': jnp.zeros((E, H), dtype=jnp.float32), 'W2': jax.random.normal(ks[3], (E, H, D), dtype=jnp.float32) * (1.0 / np.sqrt(H)), 'b2': jnp.zeros((E, D), dtype=jnp.float32)}
    _L0_ffn_in = _L0_ffn_setup()
    _d = {'L0_attn_x': _L0_attn_in['x'], 'L0_attn_W_attn': _L0_attn_in['W_attn'], 'L0_attn_b_attn': _L0_attn_in['b_attn'], 'L0_attn_W_proj': _L0_attn_in['W_proj'], 'L0_attn_b_proj': _L0_attn_in['b_proj'], 'L0_ffn_Wr': _L0_ffn_in['Wr'], 'L0_ffn_br': _L0_ffn_in['br'], 'L0_ffn_W1': _L0_ffn_in['W1'], 'L0_ffn_b1': _L0_ffn_in['b1'], 'L0_ffn_W2': _L0_ffn_in['W2'], 'L0_ffn_b2': _L0_ffn_in['b2']}
    _x0 = _d['L0_attn_x']
    _d['L0_attn_x'] = jax.random.normal(jax.random.fold_in(jax.random.key(seed), 1), (4, 1024, 128), dtype=_x0.dtype)
    del _x0
    return _d

def reference(L0_attn_x, L0_attn_W_attn, L0_attn_b_attn, L0_attn_W_proj, L0_attn_b_proj, L0_ffn_Wr, L0_ffn_br, L0_ffn_W1, L0_ffn_b1, L0_ffn_W2, L0_ffn_b2):

    def _L0_attn_ref(x, W_attn, b_attn, W_proj, b_proj):
        import jax, jax.numpy as jnp
        import numpy as np
        import math
        B, T, C = (2, 256, 128)
        NH = 16
        HD = C // NH

        def _rope_factor(T, d, dtype):
            theta = 1.0 / 10000.0 ** (2.0 * jnp.arange(0, d // 2, dtype=jnp.float32) / d)
            seq = jnp.arange(1, T + 1, dtype=jnp.float32)
            ang = jnp.einsum('n,d->nd', seq, theta)
            ang = jnp.concatenate([ang, ang], axis=-1)
            return (jnp.cos(ang) + jnp.sin(ang)).astype(dtype)
        Bs, Ts, Cs = x.shape
        qkv = x @ W_attn.T + b_attn
        q, k, v = jnp.split(qkv, 3, axis=-1)

        def to_heads(t):
            return t.reshape(Bs, Ts, NH, HD).transpose(0, 2, 1, 3)
        q, k, v = (to_heads(q), to_heads(k), to_heads(v))
        f = _rope_factor(Ts, HD, x.dtype)
        q = q * f
        k = k * f
        att = jnp.einsum('bhqd,bhkd->bhqk', q, k) * (1.0 / math.sqrt(HD))
        causal = jnp.tril(jnp.ones((Ts, Ts), dtype=bool))
        att = jnp.where(causal, att, jnp.finfo(att.dtype).min)
        att = jax.nn.softmax(att, axis=-1)
        y = jnp.einsum('bhqk,bhkd->bhqd', att, v)
        y = y.transpose(0, 2, 1, 3).reshape(Bs, Ts, Cs)
        y = y @ W_proj.T + b_proj
        return y

    def _L0_ffn_ref(x, Wr, br, W1, b1, W2, b2):
        import jax, jax.numpy as jnp
        import numpy as np
        TOP_K = 2

        def _moe(x, Wr, br, W1, b1, W2, b2):
            B, S, D = x.shape
            E = Wr.shape[1]
            xt = x.reshape(-1, D)
            logits = xt @ Wr + br
            top_vals, top_idx = jax.lax.top_k(logits, TOP_K)
            mask = jnp.zeros_like(logits, dtype=bool).at[jnp.arange(xt.shape[0])[:, None], top_idx].set(True)
            sparse_logits = jnp.where(mask, logits, -jnp.inf)
            gate = jax.nn.softmax(sparse_logits, axis=-1)
            h = jax.nn.relu(jnp.einsum('td,edh->teh', xt, W1) + b1)
            y = jnp.einsum('teh,ehd->ted', h, W2) + b2
            out = jnp.einsum('ted,te->td', y, gate)
            return out.reshape(B, S, D)
        return _moe(x, Wr, br, W1, b1, W2, b2)
    x = L0_attn_x
    x = _layernorm(x + _L0_attn_ref(x, L0_attn_W_attn, L0_attn_b_attn, L0_attn_W_proj, L0_attn_b_proj), axis=-1)
    x = _layernorm(x + _L0_ffn_ref(x, L0_ffn_Wr, L0_ffn_br, L0_ffn_W1, L0_ffn_b1, L0_ffn_W2, L0_ffn_b2), axis=-1)
    return x

_drawn_inputs = setup_inputs


def setup_inputs(seed=0):
    import zlib

    import numpy as np

    out = dict(_drawn_inputs(seed))
    spreads = {'L0_ffn_br': (0.0, 0.1), 'L0_ffn_b1': (0.0, 0.1), 'L0_ffn_b2': (0.0, 0.1)}
    factors = {'L0_attn_W_attn': 3.083}
    for name, (base, spread) in spreads.items():
        noise = np.random.default_rng([zlib.crc32(name.encode()), seed]).standard_normal(out[name].shape)
        drawn = base * np.exp(spread * noise) if base else spread * noise
        out[name] = jnp.asarray(drawn.astype(out[name].dtype))
    for name, factor in factors.items():
        out[name] = (out[name] * factor).astype(out[name].dtype)
    return out
```

```python
from contextlib import ExitStack

import concourse.bass as bass
from concourse import mybir

F32 = mybir.dt.float32
BF16 = mybir.dt.bfloat16
U32 = mybir.dt.uint32
ALU = mybir.AluOpType
ACT = mybir.ActivationFunctionType
AX = mybir.AxisListType

P = 128
B, T, C = 4, 1024, 128
NH = 16
HD = C // NH
E, H = 8, 512
QUADS = 4
HQ = NH // QUADS
TILES = T // P
N = B * T
NT = N // P
BANK = 512
PARTS = 3
GRP = 32
SHIFT_ROW = PARTS * GRP
SCALE = 1.0 / HD ** 0.5
MASKED = -1.0e30
EPS = 1e-5
STACK_DMAS = 2 * PARTS * PARTS


def max_fills():
    fills = []
    for i in range(TILES):
        keys = P * (i + 1)
        for piece, k0 in enumerate(range(0, keys, BANK)):
            w = min(BANK, keys - k0)
            per_bank = BANK // w if w <= BANK // 2 else 1
            per_bank = min(per_bank, HQ)
            heads = min(HQ, 2 * per_bank)
            for h0 in range(0, HQ, heads):
                fills.append((i, piece, h0, heads, k0, w, per_bank))
    return fills


def exp_groups():
    groups = []
    for c in range(T // BANK):
        for j in range(BANK * (c + 1) // P):
            q0 = max(P * j, BANK * c)
            w = BANK * (c + 1) - q0
            per_bank = BANK // w if w <= BANK // 2 else 1
            groups.append((c, j, q0, w, P * j >= BANK * c, min(per_bank, HQ)))
    return groups


MAX_FILLS = max_fills()
GROUPS = exp_groups()
NMAX = len(MAX_FILLS)
NG = len(GROUPS)
FILLS = [HQ // g[5] for g in GROUPS]
FILL0 = [sum(FILLS[:g]) for g in range(NG)]
NEXP = sum(FILLS)
DIAG = [g for g in range(NG) if GROUPS[g][4]]
NDIAG = len(DIAG)
LAST_OF_CHUNK = [max(g for g in range(NG) if GROUPS[g][0] == c) for c in range(2)]
PT_SLOTS = 4
LAG = 2

MAX_AFTER = [[] for _ in range(NEXP)]
for n in range(NMAX):
    MAX_AFTER[1 + n * (NEXP - 6) // NMAX].append(n)

SIDE = [
    [(2, "otr1-"), (3, "ont0-"), (4, "y0-"), (5, "ont1-"), (6, "y1-"), (8, "xt0-"), (9, "otr0"), (10, "xt1-"),
     (11, "rl-"), (11, "mt+")],
    [(2, "otr1-"), (3, "q0+"), (4, "k0+"), (5, "q1+"), (6, "k1+"), (9, "otr0"), (11, "mt+")],
    [(2, "otr1-"), (9, "otr0"), (11, "mt+")],
    [(2, "otr1-"), (4, "v0+"), (5, "v1+"), (9, "otr0"), (11, "mt+")],
]
START = ["q0+", "k0+", "q1+", "k1+", "v0+", "v1+", "mt+"]
FLUSH = ["otr1-", "ont0-", "y0-", "ont1-", "y1-", "xt0-", "xt1-", "rl-"]
SIDE_BASE = [sum(len(SIDE[p]) for p in range(q)) for q in range(QUADS)]
SIDE_N = sum(len(s) for s in SIDE)
SIDE_OFF = len(START) - sum(1 for _, j in SIDE[0] if j.endswith("-"))


def absent(b, q, job):
    if isinstance(b, int) and b == 0 and q == 0:
        return job.endswith("-")
    if isinstance(b, int) and b == B - 1:
        return job.endswith("+") and (job != "mt+" or q == QUADS - 1)
    return False


def side_at(b, q, job):
    names = [j for _, j in SIDE[q]]
    if isinstance(b, int) and b == 0 and q == 0:
        return len(START) + sum(1 for j in names[:names.index(job)] if not absent(b, q, j))
    n = b * SIDE_N + (SIDE_OFF + SIDE_BASE[q] + names.index(job))
    if isinstance(b, int) and b == B - 1:
        n -= sum(1 for p in range(q) for _, j in SIDE[p] if absent(b, p, j))
        n -= sum(1 for j in names[:names.index(job)] if absent(b, q, j))
    return n


def flush_at(job):
    last = [j for _, j in SIDE[QUADS - 1] if not absent(B - 1, QUADS - 1, j)][-1]
    return side_at(B - 1, QUADS - 1, last) + 1 + FLUSH.index(job)


def wait_apart(eng, true_by_now, *waits):
    values = [v if isinstance(v, int) else eng.to_reg(v) for _, v in waits]
    eng.wait_ge(*true_by_now)
    for (sem, _), value in zip(waits, values):
        eng.wait_ge(sem, value)


def attention(nc, ctx, x, xT, ropeT, wqkvT, bqk, bv_rows, wpT, bp_rows, wr, br_rows, x1_dram, logits):

    def sb(name, shape, dt):
        return ctx.enter_context(nc.sbuf_tensor(name, shape, dt))

    def ps(name, shape, dt):
        return ctx.enter_context(nc.psum_tensor(name, shape, dt))

    def sem(name):
        return ctx.enter_context(nc.semaphore(name))

    ident = sb("ident", [P, P], F32)
    ident_b = sb("ident_b", [P, P], BF16)
    causal = sb("causal", [P, P], BF16)
    rope = sb("rope", [P, T], F32)
    w_qkv = sb("w_qkv", [P, 3 * C], F32)
    w_p = sb("w_p", [P, C], F32)
    w_r = sb("w_r", [P, E], F32)
    b_qk = sb("b_qk", [P, 2], F32)
    b_v = sb("b_v", [P, C], F32)
    b_p = sb("b_p", [P, C], F32)
    b_r = sb("b_r", [P, E], F32)
    minus_half = sb("minus_half", [P, TILES], F32)
    x_t = sb("x_t", [P, T], F32)
    x_res = sb("x_res", [P, TILES, C], F32)
    qk = sb("qk", [P, 2, T], F32)
    rest = sb("rest", [P, BANK], F32)
    parts = sb("parts", [P, 2, PARTS, T], BF16)
    v_st = sb("v_st", [P, TILES, C], F32)
    v_aug = sb("v_aug", [P, QUADS, TILES, HQ, GRP], F32)
    q_st = [sb(f"q_st{q}", [P, HQ, T], BF16) for q in range(QUADS)]
    k_st = [sb(f"k_st{q}", [P, HQ, T], BF16) for q in range(QUADS)]
    neg = sb("neg", [P, 2, HQ, TILES], F32)
    neg_r = sb("neg_r", [P, HQ, TILES], F32)
    shift = sb("shift", [P, PARTS, HQ, TILES], BF16)
    shift_t = sb("shift_t", [PARTS * HQ * TILES, P], BF16)
    pt = sb("pt", [P, PT_SLOTS, HQ, BANK], F32)
    o_t = sb("o_t", [P, 2, BANK], F32)
    rden = sb("rden", [P, 4, HQ], F32)
    o_n = sb("o_n", [P, TILES, C], F32)
    on_t = sb("on_t", [P, 4, P], F32)
    res = sb("res", [P, TILES, C], F32)
    stats = sb("stats", [P, TILES, 6], F32)
    mv = sb("mv", [P, TILES, 2], F32)
    var_e = sb("var_e", [P, TILES], F32)
    rstd = sb("rstd", [P, TILES], F32)
    x1 = sb("x1", [P, TILES, C], F32)
    x1_t = sb("x1_t", [P, TILES, P], F32)

    ring_max = [ps(f"ring_max{i}", [P, 2 * BANK], F32) for i in range(2)]
    ring_exp = [ps(f"ring_exp{i}", [P, BANK], F32) for i in range(2)]
    o_bank = ps("o_bank", [P, BANK], F32)
    side = ps("side", [P, BANK], F32)
    side_b = side[:, 0:BANK // 2].bitcast(BF16)

    const_in = sem("const_in")
    const_set = sem("const_set")
    v_aug_set = sem("v_aug_set")
    q_clear = sem("q_clear")
    x_t_in = sem("x_t_in")
    x_res_in = sem("x_res_in")
    x_res_sum = sem("x_res_sum")
    side_full = sem("side_full")
    side_free = sem("side_free")
    high_part = sem("high_part")
    split = sem("split")
    stacked = [sem(f"stacked{q}") for q in range(QUADS)]
    v_ready = sem("v_ready")
    max_full = sem("max_full")
    max_taken = sem("max_taken")
    neg_done = sem("neg_done")
    shift_step = sem("shift_step")
    shift_split = sem("shift_split")
    shift_in = sem("shift_in")
    exp_full = sem("exp_full")
    exp_done = sem("exp_done")
    masked = sem("masked")
    pv_done = sem("pv_done")
    o_taken = sem("o_taken")
    recip_done = sem("recip_done")
    ln_step = sem("ln_step")
    var_ready = sem("var_ready")
    rstd_done = sem("rstd_done")
    x1_ready = sem("x1_ready")
    x1_out = sem("x1_out")

    NCONST = 8

    CONSTS_IN = (const_in, 16 * NCONST)
    block = ctx.enter_context(nc.Block())

    @block.sync
    def _(sp):
        for dst, src in ((w_qkv, wqkvT), (rope, ropeT), (b_qk, bqk), (b_v, bv_rows), (w_p, wpT), (b_p, bp_rows),
                         (w_r, wr), (b_r, br_rows)):
            if dst is rope:
                sp.dma_start(x_t[:, :], xT[:, 0:T]).then_inc(x_t_in, 16)
            sp.dma_start(dst[:, :], src).then_inc(const_in, 16)

        def stack(b, q):
            first = isinstance(b, int) and b == 0
            wait_apart(sp, CONSTS_IN, (split, 4 * b + 4),
                       (q_clear, q + 1) if first else (exp_full, (4 * b + q - 3) * NEXP))
            rows = slice(GRP * q, GRP * (q + 1))
            for i in range(PARTS):
                for j in range(PARTS):
                    r = GRP * i + HD * j
                    sp.dma_start(q_st[q][r:r + HD, :, :], parts[rows, 0, i, :]).then_inc(stacked[q], 16)
                    sp.dma_start(k_st[q][r:r + HD, :, :], parts[rows, 1, j, :]).then_inc(stacked[q], 16)

        def shift_rows(b, q, at):
            sp.wait_ge(side_free, at + 1)
            sp.dma_start(q_st[q][SHIFT_ROW:SHIFT_ROW + PARTS, :, :], shift_t[:, :]).then_inc(shift_in, 16)

        def store_x1(b, n):
            wait_apart(sp, CONSTS_IN, (x1_ready, n))
            sp.dma_start(x1_dram[bass.ds(b * T, T), :].rearrange("(i p) c -> p i c", p=P), x1[:, :, :])\
              .then_inc(x1_out, 16)

        def unit(b, q):
            if q == 0:
                stack(b, 3)
                if not absent(b, q, "rl-"):
                    store_x1(b - 1, 2 * b)
            if q == 1:
                if not absent(b, q, "q0+"):
                    wait_apart(sp, CONSTS_IN, (side_full, side_at(b, 0, "otr0")))
                    sp.dma_start(x_t[:, :], xT[:, bass.ds((b + 1) * T, T)]).then_inc(x_t_in, 16)
            if q == 2:
                if not (isinstance(b, int) and b == B - 1):
                    stack(b + 1, 0)
                    stack(b + 1, 1)
                wait_apart(sp, CONSTS_IN, (side_free, side_at(b, 0, "otr0") + 1))
                sp.dma_start(x_res[:, :, :], x[bass.ds(b * T, T), :].rearrange("(i p) c -> p i c", p=P))\
                  .then_inc(x_res_in, 16)
            if q == 3 and not (isinstance(b, int) and b == B - 1):
                stack(b + 1, 2)
            if not absent(b, q, "mt+"):
                shift_rows(b + (q + 1) // 4, (q + 1) % 4, side_at(b, q, "mt+"))

        for q in range(3):
            stack(0, q)
        shift_rows(0, 0, START.index("mt+"))
        unit(0, 0)
        with sp.Fori(0, B - 1) as b:
            unit(b, 1)
            unit(b, 2)
            unit(b, 3)
            unit(b + 1, 0)
        unit(B - 1, 1)
        unit(B - 1, 2)
        unit(B - 1, 3)
        store_x1(B - 1, 2 * B)
        sp.wait_ge(x1_out, 16 * B)

    def vfill_at(b):
        if isinstance(b, int) and b == 0:
            return START.index("v1+")
        return side_at(b - 1, 3, "v1+")

    @block.gpsimd
    def _(pool):
        pool.memset(ident[:, :], 0.0).then_inc(const_set, 1)
        pool.memset(causal[:, :], 0.0).then_inc(const_set, 1)
        pool.memset(minus_half[:, :], -0.5).then_inc(const_set, 1)
        pool.wait_ge(const_set, 3)
        pool.affine_select(out=ident[:, :], in_=ident[:, :], compare_op=ALU.not_equal, fill=1.0, base=0,
                           pattern=[[-1, P]], channel_multiplier=1).then_inc(const_set, 1)
        pool.affine_select(out=causal[:, :], in_=causal[:, :], compare_op=ALU.is_ge, fill=MASKED, base=0,
                           pattern=[[-1, P]], channel_multiplier=1).then_inc(const_set, 1)
        pool.wait_ge(const_set, 5)
        pool.tensor_copy(ident_b[:, :], ident[:, :]).then_inc(const_set, 1)

        def split_chunk(b, which, c, at):
            waits = [(side_free, at + 1)]
            if not (isinstance(b, int) and b == 0):
                waits += [(stacked[q], 16 * STACK_DMAS * b) for q in range(QUADS)]
            wait_apart(pool, CONSTS_IN, *waits)
            cols = slice(BANK * c, BANK * (c + 1))
            n = 3 * (4 * b + 2 * c + which)
            pool.tensor_copy(parts[:, which, 0, cols], qk[:, which, cols]).then_inc(high_part, 1)
            pool.wait_ge(high_part, n + 1)
            pool.tensor_tensor(rest[:, :], qk[:, which, cols], parts[:, which, 0, cols], ALU.subtract)\
                .then_inc(high_part, 1)
            wait_apart(pool, CONSTS_IN, (high_part, n + 2))
            pool.tensor_copy(parts[:, which, 1, cols], rest[:, :]).then_inc(high_part, 1)
            pool.wait_ge(high_part, n + 3)
            pool.tensor_tensor(parts[:, which, 2, cols], rest[:, :], parts[:, which, 1, cols], ALU.subtract)\
                .then_inc(split, 1)

        def split_shift(u, at):
            waits = [(neg_done, u + 1)]
            if not (isinstance(u, int) and u == 0):
                waits += [(shift_in, 16 * u)]
            wait_apart(pool, CONSTS_IN, *waits)
            pool.tensor_copy(shift[:, 0, :, :], neg[:, 0, :, :]).then_inc(shift_step, 1)
            pool.wait_ge(shift_step, 3 * u + 1)
            pool.tensor_tensor(neg_r[:, :, :], neg[:, 0, :, :], shift[:, 0, :, :], ALU.subtract)\
                .then_inc(shift_step, 1)
            wait_apart(pool, CONSTS_IN, (shift_step, 3 * u + 2))
            pool.tensor_copy(shift[:, 1, :, :], neg_r[:, :, :]).then_inc(shift_step, 1)
            pool.wait_ge(shift_step, 3 * u + 3)
            pool.tensor_tensor(shift[:, 2, :, :], neg_r[:, :, :], shift[:, 1, :, :], ALU.subtract)\
                .then_inc(shift_split, 1)

        def copy_v(b, q, at):
            first = isinstance(b, int) and b == 0
            wait_apart(pool, CONSTS_IN, (side_free, at + 1),
                       (v_aug_set, 2) if first else (pv_done, (4 * b + q - 3) * NG))
            pool.tensor_copy(v_aug[:, q, :, :, 0:HD],
                             v_st[:, :, GRP * q:GRP * (q + 1)].rearrange("p i (h d) -> p i h d", d=HD))\
                .then_inc(v_ready, 1)

        def mask_weights(u, g):
            c, j, q0, w, _, _ = GROUPS[g]
            wait_apart(pool, CONSTS_IN, (exp_done, u * NEXP + FILL0[g] + FILLS[g]))
            view = pt[:, g % PT_SLOTS, :, 0:P]
            pool.affine_select(out=view, in_=view, compare_op=ALU.is_ge, fill=0.0, base=0,
                               pattern=[[0, HQ], [1, P]], channel_multiplier=-1).then_inc(masked, 1)

        def inverse_std(n):
            pool.wait_ge(var_ready, n + 1)
            half = slice(0, TILES)
            pool.tensor_tensor(rstd[:, :], var_e[:, :], minus_half[:, :], ALU.pow).then_inc(rstd_done, 1)

        def unit(b, q):
            u = 4 * b + q
            for g in range(NG):
                if g in DIAG:
                    mask_weights(u, g)
                if g == 3:
                    if q == 0:
                        copy_v(b, 3, vfill_at(b))
                        if not absent(b, q, "y1-"):
                            inverse_std(b - 1)
                    if q == 1 and not absent(b, q, "q0+"):
                        for job, which, c in (("q0+", 0, 0), ("k0+", 1, 0), ("q1+", 0, 1), ("k1+", 1, 1)):
                            split_chunk(b + 1, which, c, side_at(b, q, job))
                    if q == 2:
                        pool.wait_ge(x_res_in, 16 * b + 16)
                        pool.tensor_tensor(x_res[:, :, :], x_res[:, :, :],
                                           b_p[:, :].unsqueeze(1).to_broadcast([P, TILES, C]), ALU.add)\
                            .then_inc(x_res_sum, 1)
                    if q == 3 and not absent(b, q, "v0+"):
                        for p in range(3):
                            copy_v(b + 1, p, side_at(b, q, "v1+"))
                if g == 10 and not absent(b, q, "mt+"):
                    split_shift(u + 1, side_at(b, q, "mt+"))

        for job, which, c in (("q0+", 0, 0), ("k0+", 1, 0), ("q1+", 0, 1), ("k1+", 1, 1)):
            split_chunk(0, which, c, START.index(job))
        for q in range(3):
            copy_v(0, q, START.index("v1+"))
        split_shift(0, START.index("mt+"))
        unit(0, 0)
        with pool.Fori(0, B - 1) as b:
            unit(b, 1)
            unit(b, 2)
            unit(b, 3)
            unit(b + 1, 0)
        unit(B - 1, 1)
        unit(B - 1, 2)
        unit(B - 1, 3)
        inverse_std(B - 1)

    @block.scalar
    def _(act):
        def exps(u, g):
            c, j, q0, w, _, per_bank = GROUPS[g]
            slot = g % PT_SLOTS
            for k in range(FILLS[g]):
                f = u * NEXP + FILL0[g] + k
                if k == 0 and not (isinstance(u, int) and u == 0 and g < PT_SLOTS):
                    act.wait_ge(pv_done, u * NG + g - PT_SLOTS + 1)
                act.wait_ge(exp_full, f + 1)
                act.activation(pt[:, slot, k * per_bank:(k + 1) * per_bank, 0:w],
                               ring_exp[(FILL0[g] + k) % 2][:, 0:per_bank * w].rearrange("p (h w) -> p h w", w=w),
                               ACT.Exp, scale=SCALE).then_inc(exp_done, 1)

        def take_o(u, c):
            act.wait_ge(pv_done, u * NG + LAST_OF_CHUNK[c] + 1)
            act.activation(o_t[:, c, :], o_bank[:, :], ACT.Copy).then_inc(o_taken, 1)

        def copy_out(dst, at):
            act.wait_ge(side_full, at + 1)
            act.activation(dst, side[:, :].rearrange("p (i t) -> p i t", t=P), ACT.Copy).then_inc(side_free, 1)

        def side_job(job, at):
            if job[:3] == "ont":
                copy_out(on_t[:, :, :], at)
            if job[:2] == "xt":
                half = int(job[2])
                copy_out(x1_t[:, 4 * half:4 * half + 4, :], at)

        def unit(b, q):
            u = 4 * b + q
            for g in range(NG):
                exps(u, g)
                if g == LAG - 1 and not (isinstance(b, int) and b == 0 and q == 0):
                    take_o(u - 1, 1)
                if g == LAST_OF_CHUNK[0] + LAG:
                    take_o(u, 0)
                for after, job in SIDE[q]:
                    if after == g and not absent(b, q, job):
                        side_job(job, side_at(b, q, job))

        unit(0, 0)
        with act.Fori(0, B - 1) as b:
            unit(b, 1)
            unit(b, 2)
            unit(b, 3)
            unit(b + 1, 0)
        unit(B - 1, 1)
        unit(B - 1, 2)
        unit(B - 1, 3)
        take_o(4 * B - 1, 1)
        for job in FLUSH:
            side_job(job, flush_at(job))

    @block.vector
    def _(dve):
        def clear_stacks(q):
            dve.memset(q_st[q][:, :, :].bitcast(U32), 0)
            dve.memset(k_st[q][0:SHIFT_ROW, :, :].bitcast(U32), 0)
            dve.memset(k_st[q][SHIFT_ROW:P, :, :].bitcast(U32), 0x3F803F80).then_inc(q_clear, 1)

        def reduce_fill(u, n):
            i, piece, h0, heads, k0, w, per_bank = MAX_FILLS[n]
            if n == 0 and not (isinstance(u, int) and u == 0):
                dve.wait_ge(shift_split, u)
            dve.wait_ge(max_full, u * NMAX + n + 1)
            if per_bank == 1:
                src = ring_max[n % 2][:, :].rearrange("p (h w) -> p h w", w=BANK)[:, :, 0:w]
            else:
                src = ring_max[n % 2][:, 0:heads * w].rearrange("p (h w) -> p h w", w=w)
            dve.tensor_reduce(neg[:, piece, h0:h0 + heads, i], src, AX.X, ALU.max, negate=True)\
                .then_inc(max_taken, 1)

        def combine(u):
            dve.wait_ge(max_taken, (u + 1) * NMAX)
            dve.tensor_tensor(neg[:, 0, :, 4:8], neg[:, 0, :, 4:8], neg[:, 1, :, 4:8], ALU.min).then_inc(neg_done, 1)

        def half_of(job):
            return int(job.rstrip("+-")[-1])

        def side_job(b, q, job, at):
            name = job.rstrip("+-")
            dve.wait_ge(side_full, at + 1)
            if name in ("q0", "q1", "k0", "k1"):
                which, c = "qk".index(name[0]), int(name[1])
                if not (isinstance(b, int) and b == 0):
                    dve.wait_ge(split, 4 * b)
                cols = slice(BANK * c, BANK * (c + 1))
                dve.scalar_tensor_tensor(out=qk[:, which, cols], in0=side[:, :], scalar=b_qk[:, which:which + 1],
                                         in1=rope[:, cols], op0=ALU.add, op1=ALU.mult).then_inc(side_free, 1)
            elif name in ("v0", "v1"):
                c = int(name[1])
                if not (isinstance(b, int) and b == 0):
                    dve.wait_ge(v_ready, 4 * b)
                dve.tensor_tensor(v_st[:, 4 * c:4 * c + 4, :], side[:, :].rearrange("p (i c) -> p i c", c=C),
                                  b_v[:, :].unsqueeze(1).to_broadcast([P, 4, C]), ALU.add).then_inc(side_free, 1)
            elif name == "mt":
                u = 4 * b + q
                if not (isinstance(u, int) and u == 0):
                    dve.wait_ge(shift_in, 16 * u)
                dve.tensor_copy(shift_t[:, :], side_b[0:PARTS * HQ * TILES, 0:P]).then_inc(side_free, 1)
            elif name in ("otr0", "otr1"):
                c = int(name[3])
                view = side[:, :].rearrange("p (i h d) -> p i h d", h=HQ, d=GRP)
                dve.reciprocal(rden[:, :, :], view[:, :, :, HD]).then_inc(recip_done, 1)
                dve.wait_ge(recip_done, 2 * (4 * b + q) + c + 1)
                dve.tensor_tensor(
                    o_n[:, 4 * c:4 * c + 4, GRP * q:GRP * (q + 1)].rearrange("p i (h d) -> p i h d", d=HD),
                    view[:, :, :, 0:HD], rden[:, :, :].unsqueeze(3).to_broadcast([P, 4, HQ, HD]), ALU.mult)\
                    .then_inc(side_free, 1)
            elif name in ("y0", "y1"):
                half = int(name[1])
                step = 16 * b + 8 * half
                dve.wait_ge(x_res_sum, b + 1)
                tiles = slice(4 * half, 4 * half + 4)
                dve.tensor_tensor(res[:, tiles, :], side[:, :].rearrange("p (i c) -> p i c", c=C),
                                  x_res[:, tiles, :], ALU.add).then_inc(side_free, 1)
                dve.wait_ge(side_free, at + 1)
                for i in range(4):
                    dve.bn_stats(stats[:, 4 * half + i, :], res[:, 4 * half + i, :]).then_inc(ln_step, 1)
                wait_apart(dve, CONSTS_IN, (ln_step, step + 4))
                for i in range(4):
                    dve.bn_aggr(mv[:, 4 * half + i, :], stats[:, 4 * half + i, :]).then_inc(ln_step, 1)
                if half == 1:
                    dve.wait_ge(ln_step, step + 8)
                    dve.tensor_scalar(var_e[:, :], mv[:, :, 1], EPS, None, ALU.add).then_inc(var_ready, 1)

        def normalise(b, half):
            if half == 0:
                dve.wait_ge(rstd_done, b + 1)
                if not (isinstance(b, int) and b == 0):
                    dve.wait_ge(x1_out, 16 * b)
            for i in range(4 * half, 4 * half + 4):
                ins = dve.tensor_scalar(x1[:, i, :], res[:, i, :], mv[:, i, 0:1], rstd[:, i:i + 1],
                                        ALU.subtract, ALU.mult)
            ins.then_inc(x1_ready, 1)

        def take_logits(b, at):
            dve.wait_ge(side_full, at + 1)
            dve.tensor_tensor(logits[:, bass.ds(b * TILES, TILES), :],
                              side[:, 0:TILES * E].rearrange("p (i e) -> p i e", e=E),
                              b_r[:, :].unsqueeze(1).to_broadcast([P, TILES, E]), ALU.add).then_inc(side_free, 1)

        def run_side(b, q, job, at):
            if job == "otr1-":
                pb, pq = (b - 1, 3) if q == 0 else (b, q - 1)
                side_job(pb, pq, job, at)
            elif job in ("y0-", "y1-"):
                side_job(b - 1, q, job, at)
                if job == "y1-":
                    normalise(b - 1, 0)
                    normalise(b - 1, 1)
            elif job == "rl-":
                take_logits(b - 1, at)
            elif job == "otr0":
                side_job(b, q, job, at)
            elif job == "mt+":
                side_job(b + (q + 1) // 4, (q + 1) % 4, job, at)
            elif job[0] in "qkv":
                side_job(b + 1, q, job, at)

        def unit(b, q):
            u = 4 * b + q
            has_next = not absent(b, q, "mt+")
            for g in range(NG):
                for k in range(FILLS[g]):
                    for n in MAX_AFTER[FILL0[g] + k] if has_next else []:
                        reduce_fill(u + 1, n)
                        if n == NMAX - 1:
                            combine(u + 1)
                for after, job in SIDE[q]:
                    if after == g and not absent(b, q, job):
                        run_side(b, q, job, side_at(b, q, job))

        clear_stacks(0)
        dve.wait_ge(const_in, 16 * NCONST)
        for job in START[:-1]:
            side_job(0, 0, job, START.index(job))
        dve.memset(v_aug[:, :, :, :, :], 0.0).then_inc(v_aug_set, 1)
        dve.wait_ge(v_aug_set, 1)
        dve.memset(v_aug[:, :, :, :, HD:HD + 1], 1.0).then_inc(v_aug_set, 1)
        for q in range(1, QUADS):
            clear_stacks(q)
        for n in range(NMAX):
            reduce_fill(0, n)
        combine(0)
        side_job(0, 0, "mt+", START.index("mt+"))
        unit(0, 0)
        with dve.Fori(0, B - 1) as b:
            unit(b, 1)
            unit(b, 2)
            unit(b, 3)
            unit(b + 1, 0)
        unit(B - 1, 1)
        unit(B - 1, 2)
        unit(B - 1, 3)
        for job in FLUSH:
            run_side(B, 0, job, flush_at(job))

    @block.tensor
    def _(pe):
        def fill_max(b, q, n):
            u = 4 * b + q
            i, piece, h0, heads, k0, w, per_bank = MAX_FILLS[n]
            if n == 0:
                pe.wait_ge(stacked[q], 16 * STACK_DMAS * (b + 1))
            if not (isinstance(u, int) and u == 0 and n < 2):
                pe.wait_ge(max_taken, u * NMAX + n - 1)
            diag = k0 + w == P * (i + 1)
            for h in range(heads):
                at = h * BANK if per_bank == 1 else h * w
                out = ring_max[n % 2][:, at:at + w]
                last = pe.matmul(out, q_st[q][0:SHIFT_ROW, h0 + h, P * i:P * (i + 1)],
                                 k_st[q][0:SHIFT_ROW, h0 + h, k0:k0 + w], start=True, stop=not diag)
                if diag:
                    last = pe.matmul(out[:, w - P:w], ident_b[:, :], causal[:, :], start=False, stop=True)
            last.then_inc(max_full, 1)

        def fill_exp(u, q, g, k):
            c, j, q0, w, _, per_bank = GROUPS[g]
            s = FILL0[g] + k
            if s == 0:
                pe.wait_ge(shift_in, 16 * (u + 1))
            if not (isinstance(u, int) and u == 0 and s < 2):
                pe.wait_ge(exp_done, u * NEXP + s - 1)
            for h in range(per_bank):
                last = pe.matmul(ring_exp[s % 2][:, h * w:(h + 1) * w],
                                 k_st[q][0:SHIFT_ROW + PARTS, k * per_bank + h, P * j:P * (j + 1)],
                                 q_st[q][0:SHIFT_ROW + PARTS, k * per_bank + h, q0:q0 + w], start=True, stop=True)
            last.then_inc(exp_full, 1)

        def values(u, q, g):
            c, j, q0, w, is_diag, _ = GROUPS[g]
            if g == 0:
                pe.wait_ge(v_ready, u + 1)
            if j == 0 and not (isinstance(u, int) and u == 0 and c == 0):
                pe.wait_ge(o_taken, 2 * u + c)
            pe.wait_ge(exp_done, u * NEXP + FILL0[g] + FILLS[g])
            if is_diag:
                pe.wait_ge(masked, u * NDIAG + DIAG.index(g) + 1)
            for h in range(HQ):
                last = pe.matmul(o_bank[GRP * h:GRP * (h + 1), BANK - w:BANK], v_aug[:, q, j, h, :],
                                 pt[:, g % PT_SLOTS, h, 0:w], start=j == 0, stop=g == LAST_OF_CHUNK[c])
            last.then_inc(pv_done, 1)

        def side_job(b, q, job, at):
            name = job.rstrip("+-")
            if not (isinstance(at, int) and at == 0):
                pe.wait_ge(side_free, at)
            if name in ("q0", "q1", "k0", "k1"):
                which, c = "qk".index(name[0]), int(name[1])
                pe.wait_ge(x_t_in, 16 * b + 16)
                last = pe.matmul(side[:, :], w_qkv[:, C * which:C * (which + 1)], x_t[:, BANK * c:BANK * (c + 1)],
                                 start=True, stop=True)
            elif name in ("v0", "v1"):
                for i in range(4):
                    t0 = BANK * int(name[1]) + P * i
                    last = pe.matmul(side[:, C * i:C * (i + 1)], x_t[:, t0:t0 + P], w_qkv[:, 2 * C:3 * C],
                                     start=True, stop=True)
            elif name == "mt":
                pe.wait_ge(shift_split, 4 * b + q + 1)
                last = pe.transpose(side_b[0:PARTS * HQ * TILES, 0:P],
                                    shift[:, :, :, :].rearrange("p a h i -> p (a h i)"), ident_b[:, :])
            elif name in ("otr0", "otr1"):
                c = int(name[3])
                pe.wait_ge(o_taken, 2 * (4 * b + q) + c + 1)
                for i in range(4):
                    last = pe.transpose(side[:, P * i:P * (i + 1)], o_t[:, c, P * i:P * (i + 1)], ident[:, :])
            elif name in ("ont0", "ont1"):
                for i in range(4):
                    last = pe.transpose(side[:, P * i:P * (i + 1)], o_n[:, 4 * int(name[3]) + i, :], ident[:, :])
            elif name in ("y0", "y1"):
                for i in range(4):
                    last = pe.matmul(side[:, C * i:C * (i + 1)], on_t[:, i, :], w_p[:, :], start=True, stop=True)
            elif name in ("xt0", "xt1"):
                half = int(name[2])
                pe.wait_ge(x1_ready, 2 * b + half + 1)
                for i in range(4):
                    last = pe.transpose(side[:, P * i:P * (i + 1)], x1[:, 4 * half + i, :], ident[:, :])
            elif name == "rl":
                for i in range(TILES):
                    last = pe.matmul(side[:, E * i:E * (i + 1)], x1_t[:, i, :], w_r[:, :], start=True, stop=True)
            last.then_inc(side_full, 1)

        def run_side(b, q, job, at):
            if job == "otr1-":
                u = 4 * b + q
                if q == 0:
                    side_job(b - 1, 3, job, at)
                else:
                    side_job(b, q - 1, job, at)
            elif job == "mt+":
                side_job(b + (q + 1) // 4, (q + 1) % 4, job, at)
            elif job.endswith("+"):
                side_job(b + 1, q, job, at)
            elif job.endswith("-"):
                side_job(b - 1, q, job, at)
            else:
                side_job(b, q, job, at)

        def unit(b, q):
            u = 4 * b + q
            has_next = not absent(b, q, "mt+")
            for g in range(NG):
                for k in range(FILLS[g]):
                    fill_exp(u, q, g, k)
                    for n in MAX_AFTER[FILL0[g] + k] if has_next else []:
                        fill_max(b + (q + 1) // 4, (q + 1) % 4, n)
                    if k == 0:
                        if g >= LAG:
                            values(u, q, g - LAG)
                        elif not (isinstance(b, int) and b == 0 and q == 0):
                            values(u - 1, (q - 1) % 4, NG - LAG + g)
                for after, job in SIDE[q]:
                    if after == g and not absent(b, q, job):
                        run_side(b, q, job, side_at(b, q, job))

        pe.wait_ge(const_in, 16 * NCONST)
        pe.wait_ge(const_set, 6)
        for job in START[:-1]:
            side_job(0, 0, job, START.index(job))
        for n in range(NMAX):
            fill_max(0, 0, n)
        side_job(0, 0, "mt+", START.index("mt+"))
        unit(0, 0)
        with pe.Fori(0, B - 1) as b:
            unit(b, 1)
            unit(b, 2)
            unit(b, 3)
            unit(b + 1, 0)
        unit(B - 1, 1)
        unit(B - 1, 2)
        unit(B - 1, 3)
        for g in range(NG - LAG, NG):
            values(4 * B - 1, 3, g)
        for job in FLUSH:
            run_side(B, 0, job, flush_at(job))


def experts_dense(nc, ctx, x1_dram, logits, w1T, w2T, b1T, b2, out):

    def sb(name, shape, dt):
        return ctx.enter_context(nc.sbuf_tensor(name, shape, dt))

    def ps(name, shape, dt):
        return ctx.enter_context(nc.psum_tensor(name, shape, dt))

    def sem(name):
        return ctx.enter_context(nc.semaphore(name))

    HC = H // P
    CT = BANK // P
    NC = NT // CT
    w1 = sb("w1", [P, E, H], F32)
    w2 = sb("w2", [P, E, HC, C], F32)
    b1 = sb("b1", [P, E, HC], F32)
    b2s = sb("b2s", [E, C], F32)
    ident = sb("ident2", [P, P], F32)
    iota_e = sb("iota_e", [P, E], F32)
    top = sb("top", [P, NT, 8], F32)
    topi = sb("topi", [P, NT, 8], U32)
    topf = sb("topf", [P, NT, 2], F32)
    diff = sb("diff", [P, NT], F32)
    ex = sb("ex", [P, NT], F32)
    den = sb("den", [P, NT], F32)
    g12 = sb("g12", [P, 2, NT], F32)
    hot = sb("hot", [P, 2, NT, E], F32)
    gates = sb("gates", [P, NT, E], F32)
    xin = sb("xin", [P, 2, CT, C], F32)
    xt = sb("xt", [P, BANK], F32)
    gt = sb("gt", [E, CT, P], F32)
    gchunk = sb("gchunk", [P, CT, E], F32)
    hid = sb("hid", [P, 2, HC, BANK], F32)
    acc = sb("acc", [P, 2, CT, C], F32)
    stats = sb("stats2", [P, CT, 6], F32)
    mv = sb("mv2", [P, CT, 2], F32)
    var_e = sb("var_e2", [P, CT], F32)
    rstd = sb("rstd2", [P, CT], F32)
    minus_half = sb("minus_half2", [P, CT], F32)
    y_out = sb("y_out", [P, 2, CT, C], F32)

    hp = [ps(f"hp{i}", [P, BANK], F32) for i in range(4)]
    yp = [ps(f"yp{i}", [P, BANK], F32) for i in range(2)]
    tp = ps("tp", [P, BANK], F32)
    bp = ps("bp", [P, BANK], F32)

    w_in = sem("w_in")
    const_set = sem("const_set2")
    x_in = [sem(f"x_in{s}") for s in range(2)]
    top_done = sem("top_done")
    gate_step = sem("gate_step")
    diff_done = sem("diff_done")
    ex_done = sem("ex_done")
    gates_done = sem("gates_done")
    chunk_gates = sem("chunk_gates")
    x_turned = sem("x_turned")
    xt_done = sem("xt_done")
    gt_full = sem("gt_full")
    gt_done = sem("gt_done")
    base_full = sem("base_full")
    acc_step = sem("acc_step")
    hp_full = sem("hp_full")
    hid_done = sem("hid_done")
    yp_full = sem("yp_full")
    yp_taken = sem("yp_taken")
    ln_step = sem("ln_step2")
    var_ready = sem("var_ready2")
    rstd_done = sem("rstd_done2")
    y_ready = sem("y_ready")
    y_stored = sem("y_stored")

    WEIGHTS_IN = (w_in, 16 * (2 + 2 * E))
    block = ctx.enter_context(nc.Block())

    @block.sync
    def _(sp):
        def load_x(c, slot):
            sp.dma_start(xin[:, slot, :, :], x1_dram[bass.ds(c * BANK, BANK), :].rearrange("(i p) c -> p i c", p=P))\
              .then_inc(x_in[slot], 16)

        load_x(0, 0)
        sp.dma_start(b1[:, :, :], b1T).then_inc(w_in, 16)
        sp.dma_start(b2s[:, :], b2).then_inc(w_in, 16)
        for e in range(E):
            sp.dma_start(w1[:, e, :], w1T[:, H * e:H * (e + 1)]).then_inc(w_in, 16)
            sp.dma_start(w2[:, e, :, :].rearrange("p k c -> p (k c)"), w2T[:, H * e:H * (e + 1)]).then_inc(w_in, 16)
        def pair(c2):
            for s in range(2):
                c = 2 * c2 + s
                if s == 0:
                    if not (isinstance(c, int) and c == 0):
                        wait_apart(sp, WEIGHTS_IN, (y_ready, c))
                    load_x(c + 1, 1)
                wait_apart(sp, WEIGHTS_IN, (y_ready, c + 1))
                sp.dma_start(out[bass.ds(c * BANK, BANK), :].rearrange("(i p) c -> p i c", p=P), y_out[:, s, :, :])\
                  .then_inc(y_stored, 16)
                if s == 1:
                    load_x((c + 1) % NC, 0)
        pair(0)
        with sp.Fori(1, NC // 2) as c2:
            pair(c2)
        sp.wait_ge(x_in[0], 16 * (NC // 2 + 1))
        sp.wait_ge(y_stored, 16 * NC)

    @block.gpsimd
    def _(pool):
        pool.memset(ident[:, :], 0.0).then_inc(const_set, 1)
        pool.memset(minus_half[:, :], -0.5).then_inc(const_set, 1)
        pool.iota(iota_e[:, :], pattern=[[1, E]], base=0, channel_multiplier=0,
                  allow_small_or_imprecise_dtypes=True).then_inc(const_set, 1)
        pool.wait_ge(const_set, 3)
        pool.affine_select(out=ident[:, :], in_=ident[:, :], compare_op=ALU.not_equal, fill=1.0, base=0,
                           pattern=[[-1, P]], channel_multiplier=1).then_inc(const_set, 1)
        with pool.Fori(0, NC) as c:
            pool.wait_ge(var_ready, c + 1)
            pool.tensor_tensor(rstd[:, :], var_e[:, :], minus_half[:, :], ALU.pow).then_inc(rstd_done, 1)

    @block.scalar
    def _(act):
        act.wait_ge(diff_done, 1)
        act.activation(ex[:, :], diff[:, :], ACT.Exp).then_inc(ex_done, 1)
        def chunk(c):
            act.wait_ge(x_turned, c + 1)
            act.activation(xt[:, :], tp[:, :], ACT.Copy).then_inc(xt_done, 1)
            for e in range(E):
                for k in range(HC):
                    act.wait_ge(hp_full, HC * (E * c + e) + k + 1)
                    if k == 0 and not (isinstance(c, int) and c == 0 and e < 2):
                        act.wait_ge(yp_full, E * c + e - 1)
                    act.activation(hid[:, e % 2, k, :], hp[k][:, :], ACT.Relu, bias=b1[:, e, k:k + 1])\
                        .then_inc(hid_done, 1)

        chunk(0)
        with act.Fori(1, NC) as c:
            chunk(c)

    @block.vector
    def _(dve):
        for i in range(NT):
            dve.max(top[:, i, :], logits[:, i, :]).then_inc(top_done, 1)
        dve.wait_ge(top_done, NT)
        dve.tensor_tensor(diff[:, :], top[:, :, 1], top[:, :, 0], ALU.subtract).then_inc(diff_done, 1)
        for i in range(NT):
            dve.max_index(topi[:, i, :], top[:, i, :], logits[:, i, :]).then_inc(top_done, 1)
        dve.wait_ge(top_done, 2 * NT)
        dve.tensor_copy(topf[:, :, :], topi[:, :, 0:2]).then_inc(gate_step, 1)
        dve.wait_ge(ex_done, 1)
        dve.tensor_scalar(den[:, :], ex[:, :], 1.0, None, ALU.add).then_inc(gate_step, 1)
        dve.wait_ge(gate_step, 2)
        dve.reciprocal(g12[:, 0, :], den[:, :]).then_inc(gate_step, 1)
        dve.wait_ge(gate_step, 3)
        dve.tensor_tensor(g12[:, 1, :], g12[:, 0, :], ex[:, :], ALU.mult).then_inc(gate_step, 1)
        dve.wait_ge(const_set, 4)
        for r in range(2):
            dve.tensor_tensor(hot[:, r, :, :], topf[:, :, r:r + 1].to_broadcast([P, NT, E]),
                              iota_e[:, :].unsqueeze(1).to_broadcast([P, NT, E]), ALU.is_equal).then_inc(gate_step, 1)
        dve.wait_ge(gate_step, 6)
        for r in range(2):
            dve.tensor_tensor(hot[:, r, :, :], hot[:, r, :, :], g12[:, r, :].unsqueeze(2).to_broadcast([P, NT, E]),
                              ALU.mult).then_inc(gate_step, 1)
        dve.wait_ge(gate_step, 8)
        dve.tensor_tensor(gates[:, :, :], hot[:, 0, :, :], hot[:, 1, :, :], ALU.add).then_inc(gates_done, 1)
        dve.wait_ge(gates_done, 1)
        def pair(c2):
            for s in range(2):
                c = 2 * c2 + s
                if not (isinstance(c, int) and c == 0):
                    dve.wait_ge(gt_full, c)
                dve.tensor_copy(gchunk[:, :, :], gates[:, bass.ds(CT * c, CT), :]).then_inc(chunk_gates, 1)
                dve.wait_ge(gt_full, c + 1)
                dve.tensor_copy(gt[:, :, :].rearrange("e i t -> e (i t)"), bp[0:E, :]).then_inc(gt_done, 1)
                dve.wait_ge(base_full, c + 1)
                dve.wait_ge(x_in[s], 16 * (c2 + 1))
                dve.tensor_tensor(acc[:, s, :, :], bp[:, :].rearrange("p (i c) -> p i c", c=C), xin[:, s, :, :],
                                  ALU.add).then_inc(acc_step, 1)
                for e in range(E):
                    dve.wait_ge(yp_full, E * c + e + 1)
                    dve.wait_ge(acc_step, (4 * E + 1) * c + 4 * e + 1)
                    for i in range(CT):
                        ins = dve.scalar_tensor_tensor(out=acc[:, s, i, :], in0=yp[e % 2][:, C * i:C * (i + 1)],
                                                       scalar=gchunk[:, i, e:e + 1], in1=acc[:, s, i, :],
                                                       op0=ALU.mult, op1=ALU.add)
                        ins.then_inc(acc_step, 1)
                dve.wait_ge(acc_step, (4 * E + 1) * (c + 1))
                for i in range(CT):
                    dve.bn_stats(stats[:, i, :], acc[:, s, i, :]).then_inc(ln_step, 1)
                wait_apart(dve, (gates_done, 1), (ln_step, 8 * c + 4))
                for i in range(CT):
                    dve.bn_aggr(mv[:, i, :], stats[:, i, :]).then_inc(ln_step, 1)
                dve.wait_ge(ln_step, 8 * c + 8)
                dve.tensor_scalar(var_e[:, :], mv[:, :, 1], EPS, None, ALU.add).then_inc(var_ready, 1)
                dve.wait_ge(rstd_done, c + 1)
                if not (isinstance(c2, int) and c2 == 0):
                    dve.wait_ge(y_stored, 16 * (c - 1))
                for i in range(CT):
                    ins = dve.tensor_scalar(y_out[:, s, i, :], acc[:, s, i, :], mv[:, i, 0:1], rstd[:, i:i + 1],
                                            ALU.subtract, ALU.mult)
                ins.then_inc(y_ready, 1)

        pair(0)
        with dve.Fori(1, NC // 2) as c2:
            pair(c2)

    @block.tensor
    def _(pe):
        pe.wait_ge(const_set, 4)
        pe.wait_ge(w_in, 16 * (2 + 2 * E))
        def pair(c2):
            for s in range(2):
                c = 2 * c2 + s
                pe.wait_ge(x_in[s], 16 * (c2 + 1))
                for i in range(CT):
                    last = pe.transpose(tp[:, P * i:P * (i + 1)], xin[:, s, i, :], ident[:, :])
                last.then_inc(x_turned, 1)
                pe.wait_ge(chunk_gates, c + 1)
                if not (isinstance(c, int) and c == 0):
                    pe.wait_ge(acc_step, (4 * E + 1) * c)
                for i in range(CT):
                    last = pe.transpose(bp[0:E, P * i:P * (i + 1)], gchunk[:, i, :], ident[:, :])
                last.then_inc(gt_full, 1)
                pe.wait_ge(gt_done, c + 1)
                for i in range(CT):
                    last = pe.matmul(bp[:, C * i:C * (i + 1)], gt[:, i, :], b2s[:, :], start=True, stop=True)
                last.then_inc(base_full, 1)
                pe.wait_ge(xt_done, c + 1)

                def up(e):
                    for k in range(HC):
                        if not (isinstance(c, int) and c == 0 and e == 0):
                            pe.wait_ge(hid_done, HC * (E * c + e) + k - 3)
                        pe.matmul(hp[k][:, :], w1[:, e, P * k:P * (k + 1)], xt[:, :], start=True, stop=True)\
                          .then_inc(hp_full, 1)

                def down(e):
                    pe.wait_ge(hid_done, HC * (E * c + e) + HC)
                    if e > 1:
                        pe.wait_ge(acc_step, (4 * E + 1) * c + 1 + 4 * (e - 1))
                    elif not (isinstance(c, int) and c == 0):
                        pe.wait_ge(acc_step, (4 * E + 1) * c)
                    for i in range(CT):
                        for k in range(HC):
                            last = pe.matmul(yp[e % 2][:, C * i:C * (i + 1)], hid[:, e % 2, k, P * i:P * (i + 1)],
                                             w2[:, e, k, :], start=k == 0, stop=k == HC - 1)
                    last.then_inc(yp_full, 1)

                up(0)
                for e in range(1, E):
                    up(e)
                    down(e - 1)
                down(E - 1)

        pair(0)
        with pe.Fori(1, NC // 2) as c2:
            pair(c2)


def program(nc, x, xT, ropeT, wqkvT, bqk, bv_rows, wpT, bp_rows, wr, br_rows, w1T, w2T, b1T, b2, out):
    x1_dram = nc.dram_tensor("x1_dram", (N, C), F32, kind="Internal").ap()
    with ExitStack() as outer:
        logits = outer.enter_context(nc.sbuf_tensor("logits", [P, NT, E], F32))
        with ExitStack() as ctx:
            attention(nc, ctx, x, xT, ropeT, wqkvT, bqk, bv_rows, wpT, bp_rows, wr, br_rows, x1_dram, logits)
        with ExitStack() as ctx:
            experts_dense(nc, ctx, x1_dram, logits, w1T, w2T, b1T, b2, out)


def rope_rows():
    import numpy as np

    theta = (np.float32(1.0) / np.float32(10000.0) ** (
        np.float32(2.0) * np.arange(0, HD // 2, dtype=np.float32) / np.float32(HD))).astype(np.float32)
    ang = np.arange(1, T + 1, dtype=np.float32)[None, :] * theta[:, None]
    f = (np.cos(ang) + np.sin(ang)).astype(np.float32)
    f = np.concatenate([f, f], axis=0)
    return np.tile(np.repeat(f, HQ, axis=0), (QUADS, 1))


def kernel(**inputs):
    import numpy as np
    import concourse.bacc as bacc
    from concourse.bass_utils import run_bass_kernel_spmd

    a = {k: np.asarray(v) for k, v in inputs.items()}
    x = a["L0_attn_x"].reshape(N, C)

    def by_channel(w):
        return w.reshape(QUADS, HQ, HD, -1).transpose(0, 2, 1, 3).reshape(C, -1)

    wq, wk, wv = a["L0_attn_W_attn"].reshape(3, C, C)
    bq, bk, bv = a["L0_attn_b_attn"].reshape(3, C)
    arrays = {
        "x": x,
        "xT": x.T,
        "ropeT": rope_rows(),
        "wqkvT": np.concatenate([by_channel(wq), by_channel(wk), wv]).T,
        "bqk": np.concatenate([by_channel(bq), by_channel(bk)], axis=1),
        "bv_rows": np.broadcast_to(bv, (P, C)),
        "wpT": a["L0_attn_W_proj"].T,
        "bp_rows": np.broadcast_to(a["L0_attn_b_proj"], (P, C)),
        "wr": a["L0_ffn_Wr"],
        "br_rows": np.broadcast_to(a["L0_ffn_br"], (P, E)),
        "w1T": a["L0_ffn_W1"].transpose(1, 0, 2).reshape(C, E * H),
        "w2T": a["L0_ffn_W2"].reshape(E, H // P, P, C).transpose(2, 0, 1, 3).reshape(P, E * H),
        "b1T": a["L0_ffn_b1"].reshape(E, H // P, P).transpose(2, 0, 1),
        "b2": a["L0_ffn_b2"],
    }
    arrays = {k: np.ascontiguousarray(v) for k, v in arrays.items()}
    nc = bacc.Bacc("TRN2", target_bir_lowering=False, num_devices=1)
    args = [nc.dram_tensor(f"in_{k}", v.shape, F32, kind="ExternalInput").ap() for k, v in arrays.items()]
    out = nc.dram_tensor("out_0", (N, C), F32, kind="ExternalOutput").ap()
    program(nc, *args, out)
    r = run_bass_kernel_spmd(nc, [{f"in_{k}": v for k, v in arrays.items()}], core_ids=[0])
    return r.results[0]["out_0"].reshape(B, T, C)
```

```python
from contextlib import ExitStack

import concourse.bass as bass
from concourse import mybir

F32 = mybir.dt.float32
BF16 = mybir.dt.bfloat16
U32 = mybir.dt.uint32
I32 = mybir.dt.int32
ALU = mybir.AluOpType
ACT = mybir.ActivationFunctionType
AX = mybir.AxisListType

P = 128
B, T, C = 4, 1024, 128
NH = 16
HD = C // NH
E, H = 8, 512
QUADS = 4
HQ = NH // QUADS
TILES = T // P
N = B * T
NT = N // P
BANK = 512
PARTS = 3
GRP = 32
SHIFT_ROW = PARTS * GRP
SCALE = 1.0 / HD ** 0.5
MASKED = -1.0e30
EPS = 1e-5
STACK_DMAS = 2 * PARTS * PARTS

CHOICES = 2
JR = CHOICES * TILES
BLK = 256
BT = BLK // P
REGION = N + BLK
ROW = C + 2
NBLK = 40
NOWHERE = CHOICES * N
HC = H // P
WROW = H + HC * C + HC + C
ROWS_STEP = 16 * JR


def max_fills():
    fills = []
    for i in range(TILES):
        keys = P * (i + 1)
        for piece, k0 in enumerate(range(0, keys, BANK)):
            w = min(BANK, keys - k0)
            per_bank = BANK // w if w <= BANK // 2 else 1
            for h0 in range(0, HQ, per_bank):
                fills.append((i, piece, h0, per_bank, k0, w))
    return fills


def exp_groups():
    groups = []
    for c in range(T // BANK):
        for j in range(BANK * (c + 1) // P):
            q0 = max(P * j, BANK * c)
            w = BANK * (c + 1) - q0
            per_bank = BANK // w if w <= BANK // 2 else 1
            groups.append((c, j, q0, w, P * j >= BANK * c, min(per_bank, HQ)))
    return groups


MAX_FILLS = max_fills()
GROUPS = exp_groups()
NMAX = len(MAX_FILLS)
NG = len(GROUPS)
FILLS = [HQ // g[5] for g in GROUPS]
FILL0 = [sum(FILLS[:g]) for g in range(NG)]
NEXP = sum(FILLS)
DIAG = [g for g in range(NG) if GROUPS[g][4]]
NDIAG = len(DIAG)
LAST_OF_CHUNK = [max(g for g in range(NG) if GROUPS[g][0] == c) for c in range(2)]
PT_SLOTS = 4
GATE_GROUP = 3
LAG = 2

RING = 3
AHEAD = 12
assert NMAX == NEXP


def taken_before(u, k):
    return u * NEXP + (k - RING if k >= RING else max(j for j in range(NEXP) if j % RING == k) - NEXP) + 1


def max_fill_beside(b, q, k):
    d, n = (1, k + AHEAD) if k + AHEAD < NMAX else (2, k + AHEAD - NMAX)
    if isinstance(b, int) and b == B - 1 and q + d >= QUADS:
        return None
    return b + (q + d) // QUADS, (q + d) % QUADS, n


SIDE = [
    [(2, "otr1-"), (3, "ont0-"), (4, "y0-"), (5, "ont1-"), (6, "y1-"), (7, "otr0"), (8, "mt+"), (8, "xt0-"),
     (9, "xt1-"), (11, "rl-")],
    [(2, "otr1-"), (3, "q0+"), (4, "k0+"), (5, "q1+"), (6, "k1+"), (7, "otr0"), (8, "mt+"), (9, "rk-")],
    [(2, "otr1-"), (7, "otr0"), (8, "mt+")],
    [(2, "otr1-"), (4, "v0+"), (5, "v1+"), (7, "otr0"), (8, "mt+")],
]
START = ["q0+", "k0+", "q1+", "k1+", "v0+", "v1+", "mt+"]
FLUSH = ["otr1-", "ont0-", "y0-", "ont1-", "y1-", "xt0-", "xt1-", "rl-", "rk-"]
SIDE_N = sum(len(s) for s in SIDE)


def absent(b, q, job):
    if isinstance(b, int) and b == 0:
        return job.endswith("-") and (q == 0 or job == "rk-")
    if isinstance(b, int) and b == B - 1:
        return job.endswith("+") and (job != "mt+" or q == QUADS - 1)
    return False


SIDE_ORDER = ([("start", 0, job) for job in START]
              + [(b, q, job) for b in range(B) for q in range(QUADS) for _, job in SIDE[q] if not absent(b, q, job)]
              + [("flush", 0, job) for job in FLUSH])


def side_at(b, q, job):
    if isinstance(b, int):
        return SIDE_ORDER.index((b, q, job))
    return b * SIDE_N + (SIDE_ORDER.index((1, q, job)) - SIDE_N)


def flush_at(job):
    return SIDE_ORDER.index(("flush", 0, job))


def wait_apart(eng, true_by_now, *waits):
    values = [v if isinstance(v, int) else eng.to_reg(v) for _, v in waits]
    eng.wait_ge(*true_by_now)
    for (sem, _), value in zip(waits, values):
        eng.wait_ge(sem, value)


def own_copy(eng, value):
    if isinstance(value, int):
        return value
    register = eng.alloc_register(f"copy_{eng.engine.name}")
    eng.reg_mov(register, value)
    return eng.snap(register)


def attention(nc, ctx, x, xT, ropeT, wqkvT, bqk, bv_rows, wpT, bp_rows, wr, br_rows, x1_dram, rows_dram, carry):

    def sb(name, shape, dt):
        return ctx.enter_context(nc.sbuf_tensor(name, shape, dt))

    def ps(name, shape, dt):
        return ctx.enter_context(nc.psum_tensor(name, shape, dt))

    def sem(name):
        return ctx.enter_context(nc.semaphore(name))

    ident = sb("ident", [P, P], F32)
    ident_b = sb("ident_b", [P, P], BF16)
    causal = sb("causal", [P, P], BF16)
    rope = sb("rope", [P, T], F32)
    w_qkv = sb("w_qkv", [P, 3 * C], F32)
    w_p = sb("w_p", [P, C], F32)
    w_r = sb("w_r", [P, E], F32)
    b_qk = sb("b_qk", [P, 2], F32)
    b_v = sb("b_v", [P, C], F32)
    b_p = sb("b_p", [P, C], F32)
    b_r = sb("b_r", [P, E], F32)
    minus_half = sb("minus_half", [P, TILES], F32)
    zero = sb("zero", [P, 1], F32)
    x_t = sb("x_t", [P, T], F32)
    x_res = sb("x_res", [P, TILES, C], F32)
    qk = sb("qk", [P, 2, T], F32)
    rest = sb("rest", [P, 2, T], F32)
    parts = sb("parts", [P, 2, PARTS, T], BF16)
    v_st = sb("v_st", [P, TILES, C], F32)
    v_aug = sb("v_aug", [P, QUADS, TILES, HQ, GRP], F32)
    q_st = [sb(f"q_st{q}", [P, HQ, T], BF16) for q in range(QUADS)]
    k_st = [sb(f"k_st{q}", [P, HQ, T], BF16) for q in range(QUADS)]
    neg = sb("neg", [P, 2, 2, HQ, TILES], F32)
    neg_r = sb("neg_r", [P, HQ, TILES], F32)
    shift = sb("shift", [P, PARTS, HQ, TILES], BF16)
    shift_t = sb("shift_t", [PARTS * HQ * TILES, P], BF16)
    pt = sb("pt", [P, PT_SLOTS, HQ, BANK], F32)
    o_t = sb("o_t", [P, 2, BANK], F32)
    rden = sb("rden", [P, 4, HQ], F32)
    o_n = sb("o_n", [P, TILES, C], F32)
    on_t = sb("on_t", [P, 4, P], F32)
    res = sb("res", [P, TILES, C], F32)
    stats = sb("stats", [P, TILES, 6], F32)
    mv = sb("mv", [P, TILES, 2], F32)
    var_e = sb("var_e", [P, TILES], F32)
    rstd = sb("rstd", [P, TILES], F32)
    x1 = sb("x1", [P, TILES, C], F32)
    x1_t = sb("x1_t", [P, TILES, P], F32)

    iota_e = sb("iota_e", [P, E], F32)
    dest = sb("dest", [P, JR], F32)
    tri = sb("tri", [P, P], BF16)
    ones = sb("ones", [P, P], BF16)
    logits = sb("logits", [P, TILES, E], F32)
    top = sb("top", [P, TILES, 8], F32)
    topi = sb("topi", [P, TILES, 8], U32)
    topf = sb("topf", [P, JR], F32)
    diff = sb("diff", [P, TILES], F32)
    ex = sb("ex", [P, TILES], F32)
    den = sb("den", [P, TILES], F32)
    rows = sb("rows", [P, CHOICES, TILES, ROW], F32)
    hot = sb("hot", [P, JR + 1, E], BF16)
    place = sb("place", [P, JR, E], F32)
    row_f = sb("row_f", [P, JR], F32)
    row_i = sb("row_i", [P, JR], U32)

    ring_max = [ps(f"ring_max{i}", [P, BANK], F32) for i in range(RING)]
    ring_exp = [ps(f"ring_exp{i}", [P, BANK], F32) for i in range(RING)]
    o_bank = ps("o_bank", [P, BANK], F32)
    side = ps("side", [P, BANK], F32)
    side_b = side[:, 0:BANK // 2].bitcast(BF16)

    const_in = sem("const_in")
    const_set = sem("const_set")
    v_aug_set = sem("v_aug_set")
    q_clear = sem("q_clear")
    q_clear_dve = sem("q_clear_dve")
    q_clear_act = sem("q_clear_act")
    x_t_in = sem("x_t_in")
    x_res_in = sem("x_res_in")
    x_res_sum = sem("x_res_sum")
    side_full = sem("side_full")
    side_free = sem("side_free")
    high_part = sem("high_part")
    rest_done = sem("rest_done")
    mid_part = sem("mid_part")
    split = sem("split")
    stacked = [sem(f"stacked{q}") for q in range(QUADS)]
    v_ready = sem("v_ready")
    max_full = sem("max_full")
    max_taken = sem("max_taken")
    neg_done = sem("neg_done")
    shift_step = sem("shift_step")
    shift_split = sem("shift_split")
    shift_in = sem("shift_in")
    exp_full = sem("exp_full")
    exp_done = sem("exp_done")
    masked = sem("masked")
    pv_done = sem("pv_done")
    o_taken = sem("o_taken")
    recip_done = sem("recip_done")
    ln_step = sem("ln_step")
    var_ready = sem("var_ready")
    rstd_done = sem("rstd_done")
    x1_ready = sem("x1_ready")
    x1_out = sem("x1_out")
    route_const = sem("route_const")
    rows_in = sem("rows_in")
    top_step = sem("top_step")
    diff_done = sem("diff_done")
    ex_done = sem("ex_done")
    gate_step = sem("gate_step")
    dest_step = sem("dest_step")
    hot_done = sem("hot_done")
    place_step = sem("place_step")
    row_ready = sem("row_ready")
    scattered = sem("scattered")

    NCONST = 8

    CONSTS_IN = (const_in, 16 * NCONST)
    CHUNKS = [(c, which) for c in range(T // BANK) for which in range(2)]
    block = ctx.enter_context(nc.Block())

    @block.sync
    def _(sp):
        for dst, src in ((w_qkv, wqkvT), (rope, ropeT), (b_qk, bqk), (b_v, bv_rows), (w_p, wpT), (b_p, bp_rows),
                         (w_r, wr), (b_r, br_rows)):
            if dst is rope:
                sp.dma_start(x_t[:, :], xT[:, 0:T]).then_inc(x_t_in, 16)
            sp.dma_start(dst[:, :], src).then_inc(const_in, 16)

        def stack(b, q):
            first = isinstance(b, int) and b == 0
            if first:
                sp.wait_ge(q_clear, q + 1)
                sp.wait_ge(q_clear_act if q else q_clear_dve, max(q, 1))
                sp.wait_ge(split, 4)
            else:
                wait_apart(sp, CONSTS_IN, (split, 4 * b + 4), (exp_full, (4 * b + q - 3) * NEXP))
            rows = slice(GRP * q, GRP * (q + 1))
            for i in range(PARTS):
                for j in range(PARTS):
                    r = GRP * i + HD * j
                    sp.dma_start(q_st[q][r:r + HD, :, :], parts[rows, 0, i, :]).then_inc(stacked[q], 16)
                    sp.dma_start(k_st[q][r:r + HD, :, :], parts[rows, 1, j, :]).then_inc(stacked[q], 16)

        def shift_rows(b, q, at):
            sp.wait_ge(side_free, at + 1)
            sp.dma_start(q_st[q][SHIFT_ROW:SHIFT_ROW + PARTS, :, :], shift_t[:, :]).then_inc(shift_in, 16)

        def store_x1(b, n):
            wait_apart(sp, CONSTS_IN, (x1_ready, n))
            sp.dma_start(x1_dram[bass.ds(b * T, T), :].rearrange("(i p) c -> p i c", p=P), x1[:, :, :])\
              .then_inc(x1_out, 16)

        def load_rows(b):
            waits = [(x1_out, 16 * b + 16)]
            if not (isinstance(b, int) and b == 0):
                waits += [(scattered, ROWS_STEP * b)]
            wait_apart(sp, CONSTS_IN, *waits)
            for r in range(CHOICES):
                sp.dma_start(rows[:, r, :, 0:C], x1_dram[bass.ds(b * T, T), :].rearrange("(i p) c -> p i c", p=P))\
                  .then_inc(rows_in, 16)

        def unit(b, q):
            if q == 0:
                stack(b, 3)
                if not absent(b, q, "rl-"):
                    store_x1(b - 1, 2 * b)
            if q == 1:
                if not absent(b, q, "q0+"):
                    wait_apart(sp, CONSTS_IN, (side_full, side_at(b, 0, "otr0")))
                    sp.dma_start(x_t[:, :], xT[:, bass.ds((b + 1) * T, T)]).then_inc(x_t_in, 16)
                    stack(b + 1, 0)
                if not absent(b, q, "rk-"):
                    load_rows(b - 1)
            if q == 2:
                if not (isinstance(b, int) and b == B - 1):
                    stack(b + 1, 1)
                wait_apart(sp, CONSTS_IN, (side_free, side_at(b, 0, "otr0") + 1))
                sp.dma_start(x_res[:, :, :], x[bass.ds(b * T, T), :].rearrange("(i p) c -> p i c", p=P))\
                  .then_inc(x_res_in, 16)
            if q == 3 and not (isinstance(b, int) and b == B - 1):
                stack(b + 1, 2)
            if not absent(b, q, "mt+"):
                shift_rows(b + (q + 1) // 4, (q + 1) % 4, side_at(b, q, "mt+"))

        stack(0, 0)
        stack(0, 1)
        shift_rows(0, 0, START.index("mt+"))
        stack(0, 2)
        for q in range(QUADS):
            unit(0, q)
        with sp.Fori(1, B - 1) as b:
            for q in range(QUADS):
                unit(b, q)
        for q in range(QUADS):
            unit(B - 1, q)
        store_x1(B - 1, 2 * B)
        load_rows(B - 1)

    def vfill_at(b):
        if isinstance(b, int) and b == 0:
            return START.index("v1+")
        return side_at(b - 1, 3, "v1+")

    @block.gpsimd
    def _(pool):
        pool.memset(ident[:, :], 0.0).then_inc(const_set, 1)
        pool.memset(causal[:, :], 0.0).then_inc(const_set, 1)
        pool.memset(minus_half[:, :], -0.5).then_inc(const_set, 1)
        pool.memset(zero[:, :], 0.0).then_inc(const_set, 1)
        pool.wait_ge(const_set, 4)
        pool.affine_select(out=ident[:, :], in_=ident[:, :], compare_op=ALU.not_equal, fill=1.0, base=0,
                           pattern=[[-1, P]], channel_multiplier=1).then_inc(const_set, 1)
        pool.affine_select(out=causal[:, :], in_=causal[:, :], compare_op=ALU.is_ge, fill=MASKED, base=0,
                           pattern=[[-1, P]], channel_multiplier=1).then_inc(const_set, 1)
        pool.wait_ge(const_set, 6)
        pool.tensor_copy(ident_b[:, :], ident[:, :]).then_inc(const_set, 1)

        def rest_of(b, which, c):
            n = 4 * b + 2 * c + which
            cols = slice(BANK * c, BANK * (c + 1))
            pool.wait_ge(high_part, n + 1)
            pool.tensor_tensor(rest[:, which, cols], qk[:, which, cols], parts[:, which, 0, cols], ALU.subtract)\
                .then_inc(rest_done, 1)

        def low_part(b, which, c):
            n = 4 * b + 2 * c + which
            cols = slice(BANK * c, BANK * (c + 1))
            pool.wait_ge(mid_part, n + 1)
            pool.tensor_tensor(parts[:, which, 2, cols], rest[:, which, cols], parts[:, which, 1, cols],
                               ALU.subtract).then_inc(split, 1)

        def split_shift(u, u_parity):
            old = neg[:, u_parity, 0, :, :]
            waits = [(neg_done, u + 1)]
            if not (isinstance(u, int) and u == 0):
                waits += [(shift_in, 16 * u)]
            wait_apart(pool, CONSTS_IN, *waits)
            pool.tensor_copy(shift[:, 0, :, :], old).then_inc(shift_step, 1)
            pool.wait_ge(shift_step, 3 * u + 1)
            pool.tensor_tensor(neg_r[:, :, :], old, shift[:, 0, :, :], ALU.subtract)\
                .then_inc(shift_step, 1)
            wait_apart(pool, CONSTS_IN, (shift_step, 3 * u + 2))
            pool.tensor_copy(shift[:, 1, :, :], neg_r[:, :, :]).then_inc(shift_step, 1)
            pool.wait_ge(shift_step, 3 * u + 3)
            pool.tensor_tensor(shift[:, 2, :, :], neg_r[:, :, :], shift[:, 1, :, :], ALU.subtract)\
                .then_inc(shift_split, 1)

        def copy_v(b, q, at):
            first = isinstance(b, int) and b == 0
            wait_apart(pool, CONSTS_IN, (side_free, at + 1),
                       (v_aug_set, 2) if first else (pv_done, (4 * b + q - 3) * NG))
            pool.tensor_copy(v_aug[:, q, :, :, 0:HD],
                             v_st[:, :, GRP * q:GRP * (q + 1)].rearrange("p i (h d) -> p i h d", d=HD))\
                .then_inc(v_ready, 1)

        def mask_weights(u, g):
            c, j, q0, w, _, _ = GROUPS[g]
            wait_apart(pool, CONSTS_IN, (exp_done, u * NEXP + FILL0[g] + FILLS[g]))
            view = pt[:, g % PT_SLOTS, :, 0:P]
            pool.affine_select(out=view, in_=view, compare_op=ALU.is_ge, fill=0.0, base=0,
                               pattern=[[0, HQ], [1, P]], channel_multiplier=-1).then_inc(masked, 1)

        def inverse_std(n):
            pool.wait_ge(var_ready, n + 1)
            half = slice(0, TILES)
            pool.tensor_tensor(rstd[:, :], var_e[:, :], minus_half[:, :], ALU.pow).then_inc(rstd_done, 1)

        def scatter(b, columns):
            wait_apart(pool, CONSTS_IN, (row_ready, b + 1), (rows_in, 16 * CHOICES * (b + 1)))
            for j in columns:
                pool.indirect_dma_start(rows_dram[:, :], bass.IndirectOffsetOnAxis(ap=row_i[:, j:j + 1], axis=0),
                                        rows[:, j // TILES, j % TILES, :], None).then_inc(scattered, 16)

        def unit(b, q):
            u = 4 * b + q
            for g in range(NG):
                if q == 2 and g >= NG - TILES and not absent(b, q, "rk-"):
                    first = CHOICES * (g - NG + TILES)
                    scatter(b - 1, range(first, first + CHOICES))
                if g in DIAG:
                    mask_weights(u, g)
                if g == 3:
                    if q == 0:
                        copy_v(b, 3, vfill_at(b))
                        if not absent(b, q, "y1-"):
                            inverse_std(b - 1)
                    if q == 1 and not absent(b, q, "q0+"):
                        for c, which in CHUNKS:
                            rest_of(b + 1, which, c)
                            low_part(b + 1, which, c)
                    if q == 2:
                        pool.wait_ge(x_res_in, 16 * b + 16)
                        pool.tensor_tensor(x_res[:, :, :], x_res[:, :, :],
                                           b_p[:, :].unsqueeze(1).to_broadcast([P, TILES, C]), ALU.add)\
                            .then_inc(x_res_sum, 1)
                    if q == 3 and not absent(b, q, "v0+"):
                        for p in range(3):
                            copy_v(b + 1, p, side_at(b, q, "v1+"))
                if g == 7 and not absent(b, q, "mt+"):
                    split_shift(u + 1, (q + 1) % 2)

        pool.wait_ge(const_set, 7)
        for q in range(QUADS):
            pool.memset(k_st[q][SHIFT_ROW:P, :, :].bitcast(U32), 0x3F803F80).then_inc(q_clear, 1)
        pool.wait_ge(q_clear, QUADS)
        for c, which in CHUNKS:
            rest_of(0, which, c)
            low_part(0, which, c)
        pool.wait_ge(v_aug_set, 1)
        pool.memset(v_aug[:, :, :, :, HD:HD + 1], 1.0).then_inc(v_aug_set, 1)
        for q in range(3):
            copy_v(0, q, START.index("v1+"))
        split_shift(0, 0)
        pool.iota(iota_e[:, :], pattern=[[1, E]], base=0, channel_multiplier=0,
                  allow_small_or_imprecise_dtypes=True).then_inc(route_const, 1)
        pool.iota(dest[:, :].rearrange("p (r i) -> p r i", r=CHOICES), pattern=[[N, CHOICES], [P, TILES]], base=0,
                  channel_multiplier=1, allow_small_or_imprecise_dtypes=True).then_inc(route_const, 1)
        pool.iota(carry[:, :], pattern=[[REGION, E]], base=0, channel_multiplier=0,
                  allow_small_or_imprecise_dtypes=True).then_inc(route_const, 1)
        pool.memset(ones[:, :], 1.0).then_inc(route_const, 1)
        pool.memset(hot[:, 0, :], 0.0).then_inc(route_const, 1)
        pool.wait_ge(route_const, 5)
        pool.affine_select(out=tri[:, :], in_=ones[:, :], compare_op=ALU.is_gt, fill=0.0, base=0,
                           pattern=[[1, P]], channel_multiplier=-1).then_inc(route_const, 1)
        for q in range(QUADS):
            unit(0, q)
        with pool.Fori(1, B - 1) as b:
            for q in range(QUADS):
                unit(b, q)
        for q in range(QUADS):
            unit(B - 1, q)
        inverse_std(B - 1)
        scatter(B - 1, range(JR))
        pool.wait_ge(scattered, ROWS_STEP * B)

    @block.scalar
    def _(act):
        def exps(u, g):
            c, j, q0, w, _, per_bank = GROUPS[g]
            slot = g % PT_SLOTS
            for k in range(FILLS[g]):
                f = u * NEXP + FILL0[g] + k
                if k == 0 and not (isinstance(u, int) and u == 0 and g < PT_SLOTS):
                    act.wait_ge(pv_done, u * NG + g - PT_SLOTS + 1)
                act.wait_ge(exp_full, f + 1)
                act.activation(pt[:, slot, k * per_bank:(k + 1) * per_bank, 0:w],
                               ring_exp[(FILL0[g] + k) % RING][:, 0:per_bank * w].rearrange("p (h w) -> p h w", w=w),
                               ACT.Exp, scale=SCALE).then_inc(exp_done, 1)

        def take_o(u, c):
            act.wait_ge(pv_done, u * NG + LAST_OF_CHUNK[c] + 1)
            act.activation(o_t[:, c, :], o_bank[:, :], ACT.Copy).then_inc(o_taken, 1)

        def copy_out(dst, at):
            act.wait_ge(side_full, at + 1)
            act.activation(dst, side[:, :].rearrange("p (i t) -> p i t", t=P), ACT.Copy).then_inc(side_free, 1)

        def middle_part(b, c, which):
            cols = slice(BANK * c, BANK * (c + 1))
            act.wait_ge(rest_done, 4 * b + 2 * c + which + 1)
            act.activation(parts[:, which, 1, cols], rest[:, which, cols], ACT.Copy).then_inc(mid_part, 1)

        def side_job(job, at):
            if job[:3] == "ont":
                copy_out(on_t[:, :, :], at)
            if job[:2] == "xt":
                half = int(job[2])
                copy_out(x1_t[:, 4 * half:4 * half + 4, :], at)

        def gate_exp(b):
            act.wait_ge(diff_done, b + 1)
            act.activation(ex[:, :], diff[:, :], ACT.Exp).then_inc(ex_done, 1)

        def unit(b, q):
            u = 4 * b + q
            for g in range(NG):
                exps(u, g)
                if q == 1 and g == GATE_GROUP + 1 and not absent(b, q, "rk-"):
                    gate_exp(b - 1)
                if g == LAG - 1 and not (isinstance(b, int) and b == 0 and q == 0):
                    take_o(u - 1, 1)
                if g == LAST_OF_CHUNK[0] + LAG:
                    take_o(u, 0)
                for after, job in SIDE[q]:
                    if after == g and not absent(b, q, job):
                        side_job(job, side_at(b, q, job))
                if q == 1 and 4 <= g < 8 and not absent(b, q, "q0+"):
                    middle_part(b + 1, *CHUNKS[g - 4])

        act.wait_ge(const_set, 4)
        for q in range(1, QUADS):
            for st in (q_st[q][:, :, :], k_st[q][0:SHIFT_ROW, :, :]):
                rows = st.shape[0]
                ins = act.activation(st.rearrange("p h t -> p (h t)").bitcast(F32),
                                     zero[0:rows, :].to_broadcast([rows, HQ * T // 2]), ACT.Copy)
            ins.then_inc(q_clear_act, 1)
            if q == 1:
                for c, which in CHUNKS:
                    middle_part(0, c, which)
        act.activation(v_aug[:, :, :, :, :].rearrange("p q i h d -> p (q i h d)"),
                       zero[:, :].to_broadcast([P, QUADS * TILES * HQ * GRP]), ACT.Copy).then_inc(v_aug_set, 1)
        for q in range(QUADS):
            unit(0, q)
        with act.Fori(1, B - 1) as b:
            for q in range(QUADS):
                unit(b, q)
        for q in range(QUADS):
            unit(B - 1, q)
        take_o(4 * B - 1, 1)
        for job in FLUSH:
            side_job(job, flush_at(job))
        gate_exp(B - 1)

    @block.vector
    def _(dve):
        def reduce_fill(b, q, n):
            i, piece, h0, heads, k0, w = MAX_FILLS[n]
            u = 4 * b + q
            if n == 0 and not (isinstance(u, int) and u < 2):
                dve.wait_ge(shift_split, u - 1)
            dve.wait_ge(max_full, u * NMAX + n + 1)
            dve.tensor_reduce(neg[:, q % 2, piece, h0:h0 + heads, i],
                              ring_max[n % RING][:, 0:heads * w].rearrange("p (h w) -> p h w", w=w),
                              AX.X, ALU.max, negate=True).then_inc(max_taken, 1)
            if n == NMAX - 1:
                dve.wait_ge(max_taken, (u + 1) * NMAX)
                late = neg[:, q % 2, 0, :, TILES // 2:]
                dve.tensor_tensor(late, late, neg[:, q % 2, 1, :, TILES // 2:], ALU.min).then_inc(neg_done, 1)

        def side_job(b, q, job, at):
            name = job.rstrip("+-")
            dve.wait_ge(side_full, at + 1)
            if name in ("q0", "q1", "k0", "k1"):
                which, c = "qk".index(name[0]), int(name[1])
                if not (isinstance(b, int) and b == 0):
                    dve.wait_ge(split, 4 * b)
                    for p in range(QUADS):
                        dve.wait_ge(stacked[p], 16 * STACK_DMAS * b)
                cols = slice(BANK * c, BANK * (c + 1))
                dve.scalar_tensor_tensor(out=qk[:, which, cols], in0=side[:, :], scalar=b_qk[:, which:which + 1],
                                         in1=rope[:, cols], op0=ALU.add, op1=ALU.mult).then_inc(side_free, 1)
                dve.wait_ge(side_free, at + 1)
                dve.tensor_copy(parts[:, which, 0, cols], qk[:, which, cols]).then_inc(high_part, 1)
            elif name in ("v0", "v1"):
                c = int(name[1])
                if not (isinstance(b, int) and b == 0):
                    dve.wait_ge(v_ready, 4 * b)
                dve.tensor_tensor(v_st[:, 4 * c:4 * c + 4, :], side[:, :].rearrange("p (i c) -> p i c", c=C),
                                  b_v[:, :].unsqueeze(1).to_broadcast([P, 4, C]), ALU.add).then_inc(side_free, 1)
            elif name == "mt":
                u = 4 * b + q
                if not (isinstance(u, int) and u == 0):
                    dve.wait_ge(shift_in, 16 * u)
                dve.tensor_copy(shift_t[:, :], side_b[0:PARTS * HQ * TILES, 0:P]).then_inc(side_free, 1)
            elif name in ("otr0", "otr1"):
                c = int(name[3])
                view = side[:, :].rearrange("p (i h d) -> p i h d", h=HQ, d=GRP)
                dve.reciprocal(rden[:, :, :], view[:, :, :, HD]).then_inc(recip_done, 1)
                dve.wait_ge(recip_done, 2 * (4 * b + q) + c + 1)
                dve.tensor_tensor(
                    o_n[:, 4 * c:4 * c + 4, GRP * q:GRP * (q + 1)].rearrange("p i (h d) -> p i h d", d=HD),
                    view[:, :, :, 0:HD], rden[:, :, :].unsqueeze(3).to_broadcast([P, 4, HQ, HD]), ALU.mult)\
                    .then_inc(side_free, 1)
            elif name in ("y0", "y1"):
                half = int(name[1])
                step = 16 * b + 8 * half
                dve.wait_ge(x_res_sum, b + 1)
                tiles = slice(4 * half, 4 * half + 4)
                dve.tensor_tensor(res[:, tiles, :], side[:, :].rearrange("p (i c) -> p i c", c=C),
                                  x_res[:, tiles, :], ALU.add).then_inc(side_free, 1)
                dve.wait_ge(side_free, at + 1)
                for i in range(4):
                    dve.bn_stats(stats[:, 4 * half + i, :], res[:, 4 * half + i, :]).then_inc(ln_step, 1)
                wait_apart(dve, CONSTS_IN, (ln_step, step + 4))
                for i in range(4):
                    dve.bn_aggr(mv[:, 4 * half + i, :], stats[:, 4 * half + i, :]).then_inc(ln_step, 1)
                if half == 1:
                    dve.wait_ge(ln_step, step + 8)
                    dve.tensor_scalar(var_e[:, :], mv[:, :, 1], EPS, None, ALU.add).then_inc(var_ready, 1)

        def normalise(b, half):
            if half == 0:
                dve.wait_ge(rstd_done, b + 1)
                if not (isinstance(b, int) and b == 0):
                    dve.wait_ge(x1_out, 16 * b)
            for i in range(4 * half, 4 * half + 4):
                ins = dve.tensor_scalar(x1[:, i, :], res[:, i, :], mv[:, i, 0:1], rstd[:, i:i + 1],
                                        ALU.subtract, ALU.mult)
            ins.then_inc(x1_ready, 1)

        def take_logits(b, at):
            dve.wait_ge(side_full, at + 1)
            dve.tensor_tensor(logits[:, :, :],
                              side[:, 0:TILES * E].rearrange("p (i e) -> p i e", e=E),
                              b_r[:, :].unsqueeze(1).to_broadcast([P, TILES, E]), ALU.add).then_inc(side_free, 1)

        def top_two(b):
            dve.wait_ge(route_const, 6)
            dve.wait_ge(side_free, (side_at(b + 1, 0, "rl-") if not (isinstance(b, int) and b == B - 1)
                                    else flush_at("rl-")) + 1)
            for i in range(TILES):
                dve.max(top[:, i, :], logits[:, i, :]).then_inc(top_step, 1)
            dve.wait_ge(top_step, 2 * TILES * b + TILES)
            dve.tensor_tensor(diff[:, :], top[:, :, 1], top[:, :, 0], ALU.subtract).then_inc(diff_done, 1)

        def one_hots(b):
            for i in range(TILES):
                dve.max_index(topi[:, i, :], top[:, i, :], logits[:, i, :]).then_inc(top_step, 1)
            dve.wait_ge(top_step, 2 * TILES * (b + 1))
            dve.tensor_copy(topf[:, :].rearrange("p (r i) -> p i r", r=CHOICES), topi[:, :, 0:CHOICES])\
               .then_inc(gate_step, 1)
            dve.wait_ge(gate_step, 5 * b + 1)
            dve.tensor_tensor(hot[:, 1:, :], topf[:, :].unsqueeze(2).to_broadcast([P, JR, E]),
                              iota_e[:, :].unsqueeze(1).to_broadcast([P, JR, E]), ALU.is_equal).then_inc(hot_done, 1)

        def gates(b):
            dve.wait_ge(ex_done, b + 1)
            dve.tensor_scalar(den[:, :], ex[:, :], 1.0, None, ALU.add).then_inc(gate_step, 1)
            if not (isinstance(b, int) and b == 0):
                dve.wait_ge(scattered, ROWS_STEP * b)
                dve.wait_ge(dest_step, b)
            dve.wait_ge(gate_step, 5 * b + 2)
            dve.reciprocal(rows[:, 0, :, C], den[:, :]).then_inc(gate_step, 1)
            dve.wait_ge(gate_step, 5 * b + 3)
            dve.tensor_tensor(rows[:, 1, :, C], rows[:, 0, :, C], ex[:, :], ALU.mult).then_inc(gate_step, 1)
            dve.tensor_copy(rows[:, :, :, C + 1], dest[:, :].rearrange("p (r i) -> p r i", r=CHOICES))\
               .then_inc(gate_step, 1)

        def row_numbers(b, at):
            dve.wait_ge(side_full, at + 1)
            dve.tensor_tensor(place[:, :, :], side[:, 0:JR * E].rearrange("p (j e) -> p j e", e=E),
                              carry[:, :].unsqueeze(1).to_broadcast([P, JR, E]), ALU.add).then_inc(place_step, 1)
            dve.wait_ge(place_step, 3 * b + 1)
            dve.tensor_tensor(carry[:, :], carry[:, :], side[:, JR * E:(JR + 1) * E], ALU.add).then_inc(side_free, 1)
            dve.tensor_tensor(place[:, :, :], place[:, :, :], hot[:, 1:, :], ALU.mult).then_inc(place_step, 1)
            dve.wait_ge(place_step, 3 * b + 2)
            dve.tensor_reduce(row_f[:, :], place[:, :, :], AX.X, ALU.add).then_inc(place_step, 1)
            dve.wait_ge(gate_step, 5 * b + 5)
            dve.tensor_scalar(dest[:, :], dest[:, :], float(T), None, ALU.add).then_inc(dest_step, 1)
            dve.wait_ge(place_step, 3 * b + 3)
            dve.tensor_copy(row_i[:, :], row_f[:, :]).then_inc(row_ready, 1)

        def run_side(b, q, job, at):
            if job == "rk-":
                row_numbers(b - 1, at)
            elif job == "otr1-":
                pb, pq = (b - 1, 3) if q == 0 else (b, q - 1)
                side_job(pb, pq, job, at)
            elif job in ("y0-", "y1-"):
                side_job(b - 1, q, job, at)
                if job == "y1-":
                    normalise(b - 1, 0)
                    normalise(b - 1, 1)
            elif job == "rl-":
                take_logits(b - 1, at)
            elif job == "otr0":
                side_job(b, q, job, at)
            elif job == "mt+":
                side_job(b + (q + 1) // 4, (q + 1) % 4, job, at)
            elif job[0] in "qkv":
                side_job(b + 1, q, job, at)

        def unit(b, q):
            u = 4 * b + q
            for g in range(NG):
                for k in range(FILLS[g]):
                    fill = max_fill_beside(b, q, FILL0[g] + k)
                    if fill:
                        reduce_fill(*fill)
                if q == 1 and not absent(b, q, "rk-"):
                    if g == GATE_GROUP:
                        top_two(b - 1)
                    elif g == GATE_GROUP + 1:
                        one_hots(b - 1)
                    elif g == GATE_GROUP + 3:
                        gates(b - 1)
                for after, job in SIDE[q]:
                    if after == g and not absent(b, q, job):
                        run_side(b, q, job, side_at(b, q, job))

        dve.memset(q_st[0][:, :, :].bitcast(U32), 0)
        dve.memset(k_st[0][0:SHIFT_ROW, :, :].bitcast(U32), 0).then_inc(q_clear_dve, 1)
        dve.wait_ge(const_in, 16 * NCONST)
        for job in START[:-1]:
            side_job(0, 0, job, START.index(job))
        for n in range(NMAX):
            reduce_fill(0, 0, n)
        for n in range(AHEAD):
            reduce_fill(0, 1, n)
        side_job(0, 0, "mt+", START.index("mt+"))
        for q in range(QUADS):
            unit(0, q)
        with dve.Fori(1, B - 1) as b:
            for q in range(QUADS):
                unit(b, q)
        for q in range(QUADS):
            unit(B - 1, q)
        for job in FLUSH:
            if job == "rk-":
                top_two(B - 1)
                one_hots(B - 1)
                gates(B - 1)
            run_side(B, 0, job, flush_at(job))

    @block.tensor
    def _(pe):
        def fill_max(b, q, n):
            i, piece, h0, heads, k0, w = MAX_FILLS[n]
            u = 4 * b + q
            if n == 0:
                pe.wait_ge(stacked[q], 16 * STACK_DMAS * (b + 1))
            if not (isinstance(u, int) and u == 0 and n < RING):
                pe.wait_ge(max_taken, taken_before(u, n))
            diag = k0 + w == P * (i + 1)
            for h in range(heads):
                out = ring_max[n % RING][:, h * w:(h + 1) * w]
                last = pe.matmul(out, q_st[q][0:SHIFT_ROW, h0 + h, P * i:P * (i + 1)],
                                 k_st[q][0:SHIFT_ROW, h0 + h, k0:k0 + w], start=True, stop=not diag)
                if diag:
                    last = pe.matmul(out[:, w - P:w], ident_b[:, :], causal[:, :], start=False, stop=True)
            last.then_inc(max_full, 1)

        def fill_exp(u, q, g, k):
            c, j, q0, w, _, per_bank = GROUPS[g]
            s = FILL0[g] + k
            if s == 0:
                pe.wait_ge(shift_in, 16 * (u + 1))
            if not (isinstance(u, int) and u == 0 and s < RING):
                pe.wait_ge(exp_done, taken_before(u, s))
            for h in range(per_bank):
                last = pe.matmul(ring_exp[s % RING][:, h * w:(h + 1) * w],
                                 k_st[q][0:SHIFT_ROW + PARTS, k * per_bank + h, P * j:P * (j + 1)],
                                 q_st[q][0:SHIFT_ROW + PARTS, k * per_bank + h, q0:q0 + w], start=True, stop=True)
            last.then_inc(exp_full, 1)

        def values(u, q, g):
            c, j, q0, w, is_diag, _ = GROUPS[g]
            if g == 0:
                pe.wait_ge(v_ready, u + 1)
            if j == 0 and not (isinstance(u, int) and u == 0 and c == 0):
                pe.wait_ge(o_taken, 2 * u + c)
            pe.wait_ge(exp_done, u * NEXP + FILL0[g] + FILLS[g])
            if is_diag:
                pe.wait_ge(masked, u * NDIAG + DIAG.index(g) + 1)
            for h in range(HQ):
                last = pe.matmul(o_bank[GRP * h:GRP * (h + 1), BANK - w:BANK], v_aug[:, q, j, h, :],
                                 pt[:, g % PT_SLOTS, h, 0:w], start=j == 0, stop=g == LAST_OF_CHUNK[c])
            last.then_inc(pv_done, 1)

        def side_job(b, q, job, at):
            name = job.rstrip("+-")
            if not (isinstance(at, int) and at == 0):
                pe.wait_ge(side_free, at)
            if name in ("q0", "q1", "k0", "k1"):
                which, c = "qk".index(name[0]), int(name[1])
                pe.wait_ge(x_t_in, 16 * b + 16)
                last = pe.matmul(side[:, :], w_qkv[:, C * which:C * (which + 1)], x_t[:, BANK * c:BANK * (c + 1)],
                                 start=True, stop=True)
            elif name in ("v0", "v1"):
                for i in range(4):
                    t0 = BANK * int(name[1]) + P * i
                    last = pe.matmul(side[:, C * i:C * (i + 1)], x_t[:, t0:t0 + P], w_qkv[:, 2 * C:3 * C],
                                     start=True, stop=True)
            elif name == "mt":
                pe.wait_ge(shift_split, 4 * b + q + 1)
                last = pe.transpose(side_b[0:PARTS * HQ * TILES, 0:P],
                                    shift[:, :, :, :].rearrange("p a h i -> p (a h i)"), ident_b[:, :])
            elif name in ("otr0", "otr1"):
                c = int(name[3])
                pe.wait_ge(o_taken, 2 * (4 * b + q) + c + 1)
                for i in range(4):
                    last = pe.transpose(side[:, P * i:P * (i + 1)], o_t[:, c, P * i:P * (i + 1)], ident[:, :])
            elif name in ("ont0", "ont1"):
                for i in range(4):
                    last = pe.transpose(side[:, P * i:P * (i + 1)], o_n[:, 4 * int(name[3]) + i, :], ident[:, :])
            elif name in ("y0", "y1"):
                for i in range(4):
                    last = pe.matmul(side[:, C * i:C * (i + 1)], on_t[:, i, :], w_p[:, :], start=True, stop=True)
            elif name in ("xt0", "xt1"):
                half = int(name[2])
                pe.wait_ge(x1_ready, 2 * b + half + 1)
                for i in range(4):
                    last = pe.transpose(side[:, P * i:P * (i + 1)], x1[:, 4 * half + i, :], ident[:, :])
            elif name == "rl":
                for i in range(TILES):
                    last = pe.matmul(side[:, E * i:E * (i + 1)], x1_t[:, i, :], w_r[:, :], start=True, stop=True)
            elif name == "rk":
                pe.wait_ge(route_const, 6)
                pe.wait_ge(hot_done, b + 1)
                pe.matmul(side[:, 0:(JR + 1) * E], ones[:, :], hot[:, :, :].rearrange("p j e -> p (j e)"),
                          start=True, stop=False)
                for n in range(2, JR + 1):
                    pe.matmul(side[:, n * E:(JR + 1) * E], ones[:, :],
                              hot[:, 1:JR + 2 - n, :].rearrange("p j e -> p (j e)"), start=False, stop=False)
                last = pe.matmul(side[:, 0:JR * E], tri[:, :], hot[:, 1:, :].rearrange("p j e -> p (j e)"),
                                 start=False, stop=True)
            last.then_inc(side_full, 1)

        def run_side(b, q, job, at):
            if job == "otr1-":
                u = 4 * b + q
                if q == 0:
                    side_job(b - 1, 3, job, at)
                else:
                    side_job(b, q - 1, job, at)
            elif job == "mt+":
                side_job(b + (q + 1) // 4, (q + 1) % 4, job, at)
            elif job.endswith("+"):
                side_job(b + 1, q, job, at)
            elif job.endswith("-"):
                side_job(b - 1, q, job, at)
            else:
                side_job(b, q, job, at)

        def unit(b, q, b_max):
            u = 4 * b + q
            for g in range(NG):
                for k in range(FILLS[g]):
                    fill_exp(u, q, g, k)
                    fill = max_fill_beside(b_max, q, FILL0[g] + k)
                    if fill:
                        fill_max(*fill)
                    if k == 0:
                        if g >= LAG:
                            values(u, q, g - LAG)
                        elif not (isinstance(b, int) and b == 0 and q == 0):
                            values(u - 1, (q - 1) % 4, NG - LAG + g)
                for after, job in SIDE[q]:
                    if after == g and not absent(b, q, job):
                        run_side(b, q, job, side_at(b, q, job))

        pe.wait_ge(const_in, 16 * NCONST)
        pe.wait_ge(const_set, 7)
        for job in START[:-1]:
            side_job(0, 0, job, START.index(job))
        for n in range(NMAX):
            fill_max(0, 0, n)
        for n in range(AHEAD):
            fill_max(0, 1, n)
        side_job(0, 0, "mt+", START.index("mt+"))
        for q in range(QUADS):
            unit(0, q, 0)
        with pe.Fori(1, B - 1) as b:
            b_max = own_copy(pe, b)
            for q in range(QUADS):
                unit(b, q, b_max)
        for q in range(QUADS):
            unit(B - 1, q, B - 1)
        for g in range(NG - LAG, NG):
            values(4 * B - 1, 3, g)
        for job in FLUSH:
            run_side(B, 0, job, flush_at(job))


def experts(nc, ctx, x1_dram, rows_dram, y_dram, carry, w_all, out):

    def sb(name, shape, dt):
        return ctx.enter_context(nc.sbuf_tensor(name, shape, dt))

    def ps(name, shape, dt):
        return ctx.enter_context(nc.psum_tensor(name, shape, dt))

    def sem(name):
        return ctx.enter_context(nc.semaphore(name))

    SLOTS = 8
    CT = BANK // P
    NC = NT // CT
    M = N // BLK
    ident = sb("ident2", [P, P], F32)
    pad = sb("pad", [P, BT, ROW], F32)
    first_row = sb("first_row", [P, E], F32)
    steps_m = sb("steps_m", [P, M], F32)
    block_no = sb("block_no", [P, NBLK], F32)
    count = sb("count", [P, E], F32)
    over = sb("over", [P, E, M], F32)
    blocks = sb("blocks", [P, E], F32)
    ends = sb("ends", [P, 2, E], F32)
    carry_i = sb("carry_i", [P, E], I32)
    past = sb("past", [P, NBLK, E], F32)
    past_end = sb("past_end", [P, NBLK, E], F32)
    expert_f = sb("expert_f", [P, NBLK], F32)
    start_f = sb("start_f", [P, NBLK], F32)
    used = sb("used", [P, NBLK], F32)
    nth = sb("nth", [P, NBLK], F32)
    row0_f = sb("row0_f", [P, NBLK], F32)
    table = sb("table", [P, 2, NBLK], I32)
    w = sb("w", [P, SLOTS, WROW], F32)
    xin = sb("xin", [P, SLOTS, BT, ROW], F32)
    dest_i = sb("dest_i", [P, SLOTS, BT], U32)
    xt = sb("xt", [P, 2, BLK], F32)
    hid = sb("hid", [P, 2, HC, BLK], F32)
    y_sum = sb("y_sum", [P, 2, BT, C], F32)
    y_gated = sb("y_gated", [P, SLOTS, BT, C], F32)
    x_fin = sb("x_fin", [P, 2, CT, C], F32)
    y_fin = sb("y_fin", [P, 2, CHOICES, CT, C], F32)
    acc = sb("acc", [P, 2, CT, C], F32)
    stats = sb("stats2", [P, CT, 6], F32)
    mv = sb("mv2", [P, CT, 2], F32)
    var_e = sb("var_e2", [P, CT], F32)
    rstd = sb("rstd2", [P, CT], F32)
    minus_half = sb("minus_half2", [P, CT], F32)
    y_out = sb("y_out", [P, 2, CT, C], F32)

    hp = [ps(f"hp{i}", [P, BANK], F32) for i in range(4)]
    yp = [ps(f"yp{i}", [P, BANK], F32) for i in range(2)]
    tp = [ps(f"tp{i}", [P, BANK], F32) for i in range(2)]

    const_set = sem("const_set2")
    tab_step = sem("tab_step")
    table_ready = sem("table_ready")
    padded = sem("padded")
    w_in = [sem(f"w_in{s}") for s in range(SLOTS)]
    rows_in = [sem(f"block_in{s}") for s in range(SLOTS)]
    x_turned = sem("x_turned")
    xt_done = sem("xt_done")
    hp_full = sem("hp_full")
    hid_done = sem("hid_done")
    yp_full = sem("yp_full")
    y_summed = sem("y_summed")
    dest_done = sem("dest_done")
    y_ready = sem("y_ready")
    y_written = [sem(f"y_written{s}") for s in range(SLOTS)]
    fin_in = [sem(f"fin_in{s}") for s in range(2)]
    acc_step = sem("acc_step")
    ln_step = sem("ln_step2")
    var_ready = sem("var_ready2")
    rstd_done = sem("rstd_done2")
    out_ready = sem("out_ready")
    out_stored = sem("out_stored")

    PADS = 16 * (E + 1)
    CONSTS = 6
    block = ctx.enter_context(nc.Block())

    @block.sync
    def _(sp):
        sp.wait_ge(table_ready, 1)
        for e in range(E):
            row = sp.value_load(carry_i[0:1, e:e + 1], min_val=REGION * e, max_val=REGION * e + N)
            sp.dma_start(rows_dram[bass.ds(row, BLK), :].rearrange("(j p) c -> p j c", p=P), pad[:, :, :])\
              .then_inc(padded, 16)
        sp.dma_start(rows_dram[REGION * E:REGION * E + BLK, :].rearrange("(j p) c -> p j c", p=P), pad[:, :, :])\
          .then_inc(padded, 16)

        def load(i, s):
            wrow = sp.value_load(table[0:1, 0, bass.ds(i, 1)], min_val=0, max_val=P * (E - 1))
            sp.dma_start(w[:, s, :], w_all[bass.ds(wrow, P), :]).then_inc(w_in[s], 16)
            row = sp.value_load(table[0:1, 1, bass.ds(i, 1)], min_val=0, max_val=REGION * E)
            if isinstance(i, int) and i == 0:
                sp.wait_ge(padded, PADS)
            sp.dma_start(xin[:, s, :, :], rows_dram[bass.ds(row, BLK), :].rearrange("(j p) c -> p j c", p=P))\
              .then_inc(rows_in[s], 16)

        for s in range(SLOTS):
            load(s, s)
        with sp.Fori(1, NBLK // SLOTS) as g:
            for s in range(SLOTS):
                sp.wait_ge(y_ready, SLOTS * (g - 1) + s + 1)
                load(SLOTS * g + s, s)

        def load_fin(c, slot):
            src = bass.ds(c * BANK, BANK)
            sp.dma_start(x_fin[:, slot, :, :], x1_dram[src, :].rearrange("(i p) c -> p i c", p=P))\
              .then_inc(fin_in[slot], 16)
            for r in range(CHOICES):
                sp.dma_start(y_fin[:, slot, r, :, :],
                             y_dram[bass.ds(c * BANK + r * N, BANK), :].rearrange("(i p) c -> p i c", p=P))\
                  .then_inc(fin_in[slot], 16)

        for s in range(SLOTS):
            sp.wait_ge(y_written[s], 16 * BT * (NBLK // SLOTS))
        load_fin(0, 0)
        load_fin(1, 1)

        def store(c, s):
            sp.wait_ge(out_ready, c + 1)
            sp.dma_start(out[bass.ds(c * BANK, BANK), :].rearrange("(i p) c -> p i c", p=P), y_out[:, s, :, :])\
              .then_inc(out_stored, 16)
        with sp.Fori(0, NC // 2 - 1) as c2:
            for s in range(2):
                c = 2 * c2 + s
                store(c, s)
                load_fin(c + 2, s)
        for s in range(2):
            store(NC - 2 + s, s)
        sp.wait_ge(out_stored, 16 * NC)

    @block.gpsimd
    def _(pool):
        pool.iota(first_row[:, :], pattern=[[REGION, E]], base=0, channel_multiplier=0,
                  allow_small_or_imprecise_dtypes=True).then_inc(const_set, 1)
        pool.iota(steps_m[:, :], pattern=[[BLK, M]], base=0, channel_multiplier=0,
                  allow_small_or_imprecise_dtypes=True).then_inc(const_set, 1)
        pool.iota(block_no[:, :], pattern=[[1, NBLK]], base=0, channel_multiplier=0,
                  allow_small_or_imprecise_dtypes=True).then_inc(const_set, 1)
        pool.memset(minus_half[:, :], -0.5).then_inc(const_set, 1)
        pool.memset(pad[:, :, :], 0.0).then_inc(const_set, 1)
        pool.memset(ident[:, :], 0.0).then_inc(const_set, 1)
        pool.wait_ge(const_set, 6)
        pool.memset(pad[:, :, C + 1:C + 2], float(NOWHERE)).then_inc(const_set, 1)
        pool.affine_select(out=ident[:, :], in_=ident[:, :], compare_op=ALU.not_equal, fill=1.0, base=0,
                           pattern=[[-1, P]], channel_multiplier=1).then_inc(const_set, 1)

        with pool.Fori(0, NBLK // SLOTS) as g:
            for s in range(SLOTS):
                wait_apart(pool, (const_set, 8), (y_ready, SLOTS * g + s + 1))
                for j in range(BT):
                    pool.indirect_dma_start(y_dram[:, :], bass.IndirectOffsetOnAxis(ap=dest_i[:, s, j:j + 1], axis=0),
                                            y_gated[:, s, j, :], None,
                                            bounds_check=NOWHERE - 1, oob_is_err=False).then_inc(y_written[s], 16)
        with pool.Fori(0, NC) as c:
            pool.wait_ge(var_ready, c + 1)
            pool.tensor_tensor(rstd[:, :], var_e[:, :], minus_half[:, :], ALU.pow).then_inc(rstd_done, 1)

    @block.scalar
    def _(act):
        def take_x(i, s):
            act.wait_ge(x_turned, i + 1)
            act.activation(xt[:, s % 2, :], tp[s % 2][:, 0:BLK], ACT.Copy).then_inc(xt_done, 1)

        def take_hidden(i, s):
            for k in range(HC):
                if k % 2 == 0:
                    act.wait_ge(hp_full, 2 * i + k // 2 + 1)
                act.activation(hid[:, s % 2, k, :], hp[2 * (s % 2) + k // 2][:, BLK * (k % 2):BLK * (k % 2 + 1)],
                               ACT.Relu, bias=w[:, s, H + HC * C + k:H + HC * C + k + 1]).then_inc(hid_done, 1)

        take_x(0, 0)
        with act.Fori(0, NBLK // SLOTS - 1) as g:
            for s in range(SLOTS):
                i = SLOTS * g + s
                take_x(i + 1, s + 1)
                take_hidden(i, s)
        for s in range(SLOTS):
            i = NBLK - SLOTS + s
            if s < SLOTS - 1:
                take_x(i + 1, s + 1)
            take_hidden(i, s)

    @block.vector
    def _(dve):
        dve.wait_ge(const_set, 8)
        dve.tensor_tensor(count[:, :], carry[:, :], first_row[:, :], ALU.subtract).then_inc(tab_step, 1)
        dve.tensor_copy(carry_i[:, :], carry[:, :]).then_inc(tab_step, 1)
        dve.wait_ge(tab_step, 2)
        dve.tensor_tensor(over[:, :, :], count[:, :].unsqueeze(2).to_broadcast([P, E, M]),
                          steps_m[:, :].unsqueeze(1).to_broadcast([P, E, M]), ALU.is_gt).then_inc(tab_step, 1)
        dve.wait_ge(tab_step, 3)
        dve.tensor_reduce(blocks[:, :], over[:, :, :], AX.X, ALU.add).then_inc(tab_step, 1)
        dve.wait_ge(tab_step, 4)
        dve.tensor_copy(ends[:, 0, :], blocks[:, :]).then_inc(tab_step, 1)
        at = 5
        for n in range(3):
            src, dst, by = n % 2, 1 - n % 2, 1 << n
            dve.wait_ge(tab_step, at)
            dve.tensor_copy(ends[:, dst, 0:by], ends[:, src, 0:by]).then_inc(tab_step, 1)
            dve.tensor_tensor(ends[:, dst, by:], ends[:, src, by:], ends[:, src, :E - by], ALU.add)\
               .then_inc(tab_step, 1)
            at += 2
        dve.wait_ge(tab_step, at)
        blocks_shape = [P, NBLK, E]
        dve.tensor_tensor(past[:, :, :], block_no[:, :].unsqueeze(2).to_broadcast(blocks_shape),
                          ends[:, 1, :].unsqueeze(1).to_broadcast(blocks_shape), ALU.is_ge).then_inc(tab_step, 1)
        dve.wait_ge(tab_step, at + 1)
        dve.tensor_tensor(past_end[:, :, :], past[:, :, :], ends[:, 1, :].unsqueeze(1).to_broadcast(blocks_shape),
                          ALU.mult).then_inc(tab_step, 1)
        dve.tensor_reduce(expert_f[:, :], past[:, :, :], AX.X, ALU.add).then_inc(tab_step, 1)
        dve.wait_ge(tab_step, at + 3)
        dve.tensor_reduce(start_f[:, :], past_end[:, :, :], AX.X, ALU.max).then_inc(tab_step, 1)
        dve.tensor_scalar(used[:, :], expert_f[:, :], float(E), float(BLK), ALU.is_lt, ALU.mult).then_inc(tab_step, 1)
        dve.tensor_scalar(table[:, 0, :], expert_f[:, :], float(E - 1), float(P), ALU.min, ALU.mult)\
           .then_inc(tab_step, 1)
        dve.wait_ge(tab_step, at + 6)
        dve.tensor_tensor(nth[:, :], block_no[:, :], start_f[:, :], ALU.subtract).then_inc(tab_step, 1)
        dve.wait_ge(tab_step, at + 7)
        dve.tensor_tensor(nth[:, :], nth[:, :], used[:, :], ALU.mult).then_inc(tab_step, 1)
        dve.tensor_scalar(row0_f[:, :], expert_f[:, :], float(REGION), None, ALU.mult).then_inc(tab_step, 1)
        dve.wait_ge(tab_step, at + 9)
        dve.tensor_tensor(table[:, 1, :], row0_f[:, :], nth[:, :], ALU.add).then_inc(table_ready, 1)

        def finish(g, i, s):
            if not (isinstance(g, int) and g == 0):
                dve.wait_ge(y_written[s], 16 * BT * g)
            dve.wait_ge(rows_in[s], 16 * (g + 1))
            dve.tensor_copy(dest_i[:, s, :], xin[:, s, :, C + 1]).then_inc(dest_done, 1)
            dve.wait_ge(yp_full, i + 1)
            dve.tensor_tensor(y_sum[:, s % 2, :, :], yp[s % 2][:, 0:BT * C].rearrange("p (j c) -> p j c", c=C),
                              w[:, s, H + HC * C + HC:].unsqueeze(1).to_broadcast([P, BT, C]), ALU.add)\
               .then_inc(y_summed, 1)
            dve.wait_ge(y_summed, i + 1)
            dve.wait_ge(dest_done, i + 1)
            dve.tensor_tensor(y_gated[:, s, :, :], y_sum[:, s % 2, :, :],
                              xin[:, s, :, C:C + 1].to_broadcast([P, BT, C]), ALU.mult).then_inc(y_ready, 1)

        for s in range(SLOTS):
            finish(0, s, s)
        with dve.Fori(1, NBLK // SLOTS) as g:
            for s in range(SLOTS):
                finish(g, SLOTS * g + s, s)

        def chunk(c2, c, s):
            dve.wait_ge(fin_in[s], 16 * (1 + CHOICES) * (c2 + 1))
            dve.tensor_tensor(acc[:, s, :, :], x_fin[:, s, :, :], y_fin[:, s, 0, :, :], ALU.add).then_inc(acc_step, 1)
            dve.wait_ge(acc_step, 2 * c + 1)
            dve.tensor_tensor(acc[:, s, :, :], acc[:, s, :, :], y_fin[:, s, 1, :, :], ALU.add).then_inc(acc_step, 1)
            dve.wait_ge(acc_step, 2 * c + 2)
            for k in range(CT):
                dve.bn_stats(stats[:, k, :], acc[:, s, k, :]).then_inc(ln_step, 1)
            wait_apart(dve, (const_set, 8), (ln_step, 8 * c + 4))
            for k in range(CT):
                dve.bn_aggr(mv[:, k, :], stats[:, k, :]).then_inc(ln_step, 1)
            dve.wait_ge(ln_step, 8 * c + 8)
            dve.tensor_scalar(var_e[:, :], mv[:, :, 1], EPS, None, ALU.add).then_inc(var_ready, 1)
            dve.wait_ge(rstd_done, c + 1)
            if not (isinstance(c2, int) and c2 == 0):
                dve.wait_ge(out_stored, 16 * (c - 1))
            for k in range(CT):
                ins = dve.tensor_scalar(y_out[:, s, k, :], acc[:, s, k, :], mv[:, k, 0:1], rstd[:, k:k + 1],
                                        ALU.subtract, ALU.mult)
            ins.then_inc(out_ready, 1)

        for s in range(2):
            chunk(0, s, s)
        with dve.Fori(1, NC // 2) as c2:
            for s in range(2):
                chunk(c2, 2 * c2 + s, s)

    @block.tensor
    def _(pe):
        def turn(g, i, s):
            pe.wait_ge(rows_in[s], 16 * (g + 1))
            for j in range(BT):
                ins = pe.transpose(tp[s % 2][:, P * j:P * (j + 1)], xin[:, s, j, 0:C], ident[:, :])
            ins.then_inc(x_turned, 1)

        def up(g, i, s):
            pe.wait_ge(w_in[s], 16 * (g + 1))
            pe.wait_ge(xt_done, i + 1)
            if not (isinstance(i, int) and i < 2):
                pe.wait_ge(hid_done, HC * (i - 1))
            for k in range(HC):
                ins = pe.matmul(hp[2 * (s % 2) + k // 2][:, BLK * (k % 2):BLK * (k % 2 + 1)],
                                w[:, s, P * k:P * (k + 1)], xt[:, s % 2, :], start=True, stop=True)
                if k % 2:
                    ins.then_inc(hp_full, 1)

        def down(i, s):
            pe.wait_ge(hid_done, HC * (i + 1))
            if not (isinstance(i, int) and i < 2):
                pe.wait_ge(y_summed, i - 1)
            for j in range(BT):
                for k in range(HC):
                    ins = pe.matmul(yp[s % 2][:, C * j:C * (j + 1)], hid[:, s % 2, k, P * j:P * (j + 1)],
                                    w[:, s, H + C * k:H + C * (k + 1)], start=k == 0, stop=k == HC - 1)
            ins.then_inc(yp_full, 1)

        def step(g, s):
            i = SLOTS * g + s
            if s < SLOTS - 1:
                turn(g, i + 1, s + 1)
            elif not (isinstance(g, int) and g == NBLK // SLOTS - 1):
                turn(g + 1, i + 1, 0)
            up(g, i, s)
            if not (isinstance(i, int) and i == 0):
                down(i - 1, (s - 1) % SLOTS)

        pe.wait_ge(const_set, 8)
        turn(0, 0, 0)
        for s in range(SLOTS):
            step(0, s)
        with pe.Fori(1, NBLK // SLOTS - 1) as g:
            for s in range(SLOTS):
                step(g, s)
        for s in range(SLOTS):
            step(NBLK // SLOTS - 1, s)
        down(NBLK - 1, SLOTS - 1)


def program(nc, x, xT, ropeT, wqkvT, bqk, bv_rows, wpT, bp_rows, wr, br_rows, w_all, out):
    x1_dram = nc.dram_tensor("x1_dram", (N, C), F32, kind="Internal").ap()
    rows_dram = nc.dram_tensor("rows_dram", (REGION * E + BLK, ROW), F32, kind="Internal").ap()
    y_dram = nc.dram_tensor("y_dram", (CHOICES * N, C), F32, kind="Internal").ap()
    with ExitStack() as outer:
        carry = outer.enter_context(nc.sbuf_tensor("carry", [P, E], F32))
        with ExitStack() as ctx:
            attention(nc, ctx, x, xT, ropeT, wqkvT, bqk, bv_rows, wpT, bp_rows, wr, br_rows, x1_dram, rows_dram,
                      carry)
        with ExitStack() as ctx:
            experts(nc, ctx, x1_dram, rows_dram, y_dram, carry, w_all, out)


def rope_rows():
    import numpy as np

    theta = (np.float32(1.0) / np.float32(10000.0) ** (
        np.float32(2.0) * np.arange(0, HD // 2, dtype=np.float32) / np.float32(HD))).astype(np.float32)
    ang = np.arange(1, T + 1, dtype=np.float32)[None, :] * theta[:, None]
    f = (np.cos(ang) + np.sin(ang)).astype(np.float32)
    f = np.concatenate([f, f], axis=0)
    return np.tile(np.repeat(f, HQ, axis=0), (QUADS, 1))


def kernel(**inputs):
    import numpy as np
    import concourse.bacc as bacc
    from concourse.bass_utils import run_bass_kernel_spmd

    a = {k: np.asarray(v) for k, v in inputs.items()}
    x = a["L0_attn_x"].reshape(N, C)

    def by_channel(w):
        return w.reshape(QUADS, HQ, HD, -1).transpose(0, 2, 1, 3).reshape(C, -1)

    wq, wk, wv = a["L0_attn_W_attn"].reshape(3, C, C)
    bq, bk, bv = a["L0_attn_b_attn"].reshape(3, C)
    arrays = {
        "x": x,
        "xT": x.T,
        "ropeT": rope_rows(),
        "wqkvT": np.concatenate([by_channel(wq), by_channel(wk), wv]).T,
        "bqk": np.concatenate([by_channel(bq), by_channel(bk)], axis=1),
        "bv_rows": np.broadcast_to(bv, (P, C)),
        "wpT": a["L0_attn_W_proj"].T,
        "bp_rows": np.broadcast_to(a["L0_attn_b_proj"], (P, C)),
        "wr": a["L0_ffn_Wr"],
        "br_rows": np.broadcast_to(a["L0_ffn_br"], (P, E)),
        "w_all": np.concatenate([
            a["L0_ffn_W1"],
            a["L0_ffn_W2"].reshape(E, HC, P, C).transpose(0, 2, 1, 3).reshape(E, P, HC * C),
            a["L0_ffn_b1"].reshape(E, HC, P).transpose(0, 2, 1),
            np.broadcast_to(a["L0_ffn_b2"][:, None, :], (E, P, C)),
        ], axis=2).reshape(E * P, WROW),
    }
    arrays = {k: np.ascontiguousarray(v) for k, v in arrays.items()}
    nc = bacc.Bacc("TRN2", target_bir_lowering=False, num_devices=1)
    args = [nc.dram_tensor(f"in_{k}", v.shape, F32, kind="ExternalInput").ap() for k, v in arrays.items()]
    out = nc.dram_tensor("out_0", (N, C), F32, kind="ExternalOutput").ap()
    program(nc, *args, out)
    r = run_bass_kernel_spmd(nc, [{f"in_{k}": v for k, v in arrays.items()}], core_ids=[0])
    return r.results[0]["out_0"].reshape(B, T, C)
```

```python
from contextlib import ExitStack

import concourse.bass as bass
from concourse import mybir

F32 = mybir.dt.float32
BF16 = mybir.dt.bfloat16
U32 = mybir.dt.uint32
I32 = mybir.dt.int32
ALU = mybir.AluOpType
ACT = mybir.ActivationFunctionType
AX = mybir.AxisListType

P = 128
B, T, C = 4, 1024, 128
NH = 16
HD = C // NH
E, H = 8, 512
QUADS = 4
HQ = NH // QUADS
TILES = T // P
N = B * T
NT = N // P
BANK = 512
PARTS = 3
GRP = 32
SHIFT_ROW = PARTS * GRP
SCALE = 1.0 / HD ** 0.5
MASKED = -1.0e30
EPS = 1e-5
STACK_DMAS = 2 * PARTS * PARTS

CHOICES = 2
HT = TILES // 2
JR = CHOICES * HT
BLK = 256
BT = BLK // P
REGION = N + BLK
ROW = C + 2
NBLK = (CHOICES * N + E * (BLK - 1)) // BLK
NOWHERE = CHOICES * N
HC = H // P
WROW = H + HC * C + HC + C
ROWS_STEP = 16 * JR
MOST = N // BLK
ROUTE_CONSTS = 11


def max_fills():
    fills = []
    for i in range(TILES):
        keys = P * (i + 1)
        for piece, k0 in enumerate(range(0, keys, BANK)):
            w = min(BANK, keys - k0)
            per_bank = BANK // w if w <= BANK // 2 else 1
            for h0 in range(0, HQ, per_bank):
                fills.append((i, piece, h0, per_bank, k0, w))
    return fills


def exp_groups():
    groups = []
    for c in range(T // BANK):
        for j in range(BANK * (c + 1) // P):
            q0 = max(P * j, BANK * c)
            w = BANK * (c + 1) - q0
            per_bank = BANK // w if w <= BANK // 2 else 1
            groups.append((c, j, q0, w, P * j >= BANK * c, min(per_bank, HQ)))
    return groups


MAX_FILLS = max_fills()
GROUPS = exp_groups()
NMAX = len(MAX_FILLS)
NG = len(GROUPS)
FILLS = [HQ // g[5] for g in GROUPS]
FILL0 = [sum(FILLS[:g]) for g in range(NG)]
NEXP = sum(FILLS)
DIAG = [g for g in range(NG) if GROUPS[g][4]]
NDIAG = len(DIAG)
LAST_OF_CHUNK = [max(g for g in range(NG) if GROUPS[g][0] == c) for c in range(2)]
PT_SLOTS = 4
SCATTERS = {(2, 4): (0, 1), (2, 5): (2, 3), (2, 6): (4, 5), (2, 7): (6, 7), (2, 8): (8,), (2, 9): (9,),
            (2, 10): (10,), (3, 4): (11,), (3, 5): (12,), (3, 6): (13,), (3, 8): (14,), (3, 9): (15,)}
TOP_TWO = [(0, 7), (1, 1)]
ONE_HOTS = [(0, 8), (1, 2)]
GATE_EXP = [(0, 8), (1, 2)]
GATES = [(0, 9), (1, 3)]
MIDDLE_PARTS = [5, 6, 7, 9]
INVERSE_STD = [(3, 11), (0, 6)]
NORMALISE = [(0, 1), (0, 7)]
LAG = 2
VALUES_AFTER = 2

RING_MAX = 3
RING_EXP = 3
MT_AFTER = 4
AHEAD = 12
assert NMAX == NEXP


def taken_before(u, k, ring):
    return u * NEXP + (k - ring if k >= ring else max(j for j in range(NEXP) if j % ring == k) - NEXP) + 1


def max_fill_beside(b, q, k):
    d, n = (1, k + AHEAD) if k + AHEAD < NMAX else (2, k + AHEAD - NMAX)
    if isinstance(b, int) and b == B - 1 and q + d >= QUADS:
        return None
    return b + (q + d) // QUADS, (q + d) % QUADS, n


SIDE = [
    [(2, "xt0-"), (3, "otr1-"), (4, "ont1-"), (5, "y1-"), (6, "rl0-"), (7, "otr0"), (8, "mt+"), (9, "xt1-"),
     (11, "rk0-")],
    [(0, "rl1-"), (2, "otr1-"), (4, "q0+"), (5, "k0+"), (6, "q1+"), (7, "k1+"), (8, "mt+"), (9, "otr0"),
     (11, "rk1-")],
    [(2, "otr1-"), (7, "otr0"), (8, "mt+")],
    [(2, "otr1-"), (4, "v0+"), (5, "v1+"), (7, "otr0"), (8, "mt+"), (9, "ont0"), (10, "y0")],
]
START = ["q0+", "k0+", "q1+", "k1+", "v0+", "v1+", "mt+"]
FLUSH = ["otr1-", "xt0-", "ont1-", "rl0-", "y1-", "rk0-", "xt1-", "rl1-", "rk1-"]
SIDE_N = sum(len(s) for s in SIDE)


def absent(b, q, job):
    if isinstance(b, int) and b == 0:
        return job.endswith("-") and (q == 0 or job in ("rl1-", "rk1-"))
    if isinstance(b, int) and b == B - 1:
        return job.endswith("+") and (job != "mt+" or q == QUADS - 1)
    return False


SIDE_ORDER = ([("start", 0, job) for job in START]
              + [(b, q, job) for b in range(B) for q in range(QUADS) for _, job in SIDE[q] if not absent(b, q, job)]
              + [("flush", 0, job) for job in FLUSH])


def side_at(b, q, job):
    if isinstance(b, int):
        return SIDE_ORDER.index((b, q, job))
    return b * SIDE_N + (SIDE_ORDER.index((1, q, job)) - SIDE_N)


def flush_at(job):
    return SIDE_ORDER.index(("flush", 0, job))


def wait_apart(eng, true_by_now, *waits):
    values = [v if isinstance(v, int) else eng.to_reg(v) for _, v in waits]
    eng.wait_ge(*true_by_now)
    for (sem, _), value in zip(waits, values):
        eng.wait_ge(sem, value)


def own_copy(eng, value):
    if isinstance(value, int):
        return value
    register = eng.alloc_register(f"copy_{eng.engine.name}")
    eng.reg_mov(register, value)
    return eng.snap(register)


def attention(nc, ctx, x, xT, ropeT, wqkvT, bqk, bv_rows, wpT, bp_rows, wr, br_rows, x1_dram, rows_dram, carry, table):

    def sb(name, shape, dt):
        return ctx.enter_context(nc.sbuf_tensor(name, shape, dt))

    def ps(name, shape, dt):
        return ctx.enter_context(nc.psum_tensor(name, shape, dt))

    def sem(name):
        return ctx.enter_context(nc.semaphore(name))

    ident = sb("ident", [P, P], F32)
    ident_b = sb("ident_b", [P, P], BF16)
    causal = sb("causal", [P, P], BF16)
    rope = sb("rope", [P, T], F32)
    w_qkv = sb("w_qkv", [P, 3 * C], F32)
    w_p = sb("w_p", [P, C], F32)
    w_r = sb("w_r", [P, E], F32)
    b_qk = sb("b_qk", [P, 2], F32)
    b_v = sb("b_v", [P, C], F32)
    b_p = sb("b_p", [P, C], F32)
    b_r = sb("b_r", [P, E], F32)
    minus_half = sb("minus_half", [P, TILES], F32)
    zero = sb("zero", [P, 1], F32)
    x_t = sb("x_t", [P, T], F32)
    x_res = sb("x_res", [P, TILES, C], F32)
    qk = sb("qk", [P, 2, T], F32)
    rest = sb("rest", [P, 2, T], F32)
    parts = sb("parts", [P, 2, PARTS, T], BF16)
    v_st = sb("v_st", [P, TILES, C], F32)
    v_aug = sb("v_aug", [P, QUADS, TILES, HQ, GRP], F32)
    q_st = [sb(f"q_st{q}", [P, HQ, T], BF16) for q in range(QUADS)]
    k_st = [sb(f"k_st{q}", [P, HQ, T], BF16) for q in range(QUADS)]
    neg = sb("neg", [P, 2, 2, HQ, TILES], F32)
    neg_r = sb("neg_r", [P, HQ, TILES], F32)
    shift = sb("shift", [P, PARTS, HQ, TILES], BF16)
    shift_t = sb("shift_t", [PARTS * HQ * TILES, P], BF16)
    pt = sb("pt", [P, PT_SLOTS, HQ, BANK], F32)
    o_t = sb("o_t", [P, 2, BANK], F32)
    rden = sb("rden", [P, 4, HQ], F32)
    o_n = sb("o_n", [P, TILES, C], F32)
    on_t = sb("on_t", [P, 4, P], F32)
    res = sb("res", [P, TILES, C], F32)
    stats = sb("stats", [P, TILES, 6], F32)
    mv = sb("mv", [P, TILES, 2], F32)
    var_e = sb("var_e", [P, TILES], F32)
    rstd = sb("rstd", [P, TILES], F32)
    x1 = sb("x1", [P, TILES, C], F32)
    x1_t = sb("x1_t", [P, TILES, P], F32)

    iota_e = sb("iota_e", [P, E], F32)
    dest = sb("dest", [P, JR], F32)
    tri = sb("tri", [P, P], BF16)
    ones = sb("ones", [P, P], BF16)
    logits = sb("logits", [P, HT, E], F32)
    top = sb("top", [P, HT, 8], F32)
    topi = sb("topi", [P, HT, 8], U32)
    topf = sb("topf", [P, JR], F32)
    diff = sb("diff", [P, HT], F32)
    ex = sb("ex", [P, HT], F32)
    den = sb("den", [P, HT], F32)
    rows = sb("rows", [P, 2, CHOICES, HT, ROW], F32)
    hot = sb("hot", [P, JR + 1, E], BF16)
    place = sb("place", [P, JR, E], F32)
    row_f = sb("row_f", [P, JR], F32)
    row_i = sb("row_i", [P, 2, JR], U32)

    pad = sb("pad", [P, BT, ROW], F32)
    first_row = sb("first_row", [P, E], F32)
    steps_m = sb("steps_m", [P, MOST], F32)
    block_no = sb("block_no", [P, NBLK], F32)
    count = sb("count", [P, E], F32)
    over = sb("over", [P, E, MOST], F32)
    blocks = sb("blocks", [P, E], F32)
    ends = sb("ends", [P, 2, E], F32)
    carry_i = sb("carry_i", [P, E], I32)
    past = sb("past", [P, NBLK, E], F32)
    past_end = sb("past_end", [P, NBLK, E], F32)
    expert_f = sb("expert_f", [P, NBLK], F32)
    start_f = sb("start_f", [P, NBLK], F32)
    used = sb("used", [P, NBLK], F32)
    nth = sb("nth", [P, NBLK], F32)
    row0_f = sb("row0_f", [P, NBLK], F32)

    ring_max = [ps(f"ring_max{i}", [P, BANK], F32) for i in range(RING_MAX)]
    ring_exp = [ps(f"ring_exp{i}", [P, BANK], F32) for i in range(RING_EXP)]
    o_bank = ps("o_bank", [P, BANK], F32)
    side = ps("side", [P, BANK], F32)
    side_b = side[:, 0:BANK // 2].bitcast(BF16)
    start_banks = [*ring_exp, o_bank]

    def side_bank(at):
        return start_banks[at] if isinstance(at, int) and at < len(start_banks) else side

    const_in = sem("const_in")
    const_set = sem("const_set")
    v_aug_set = sem("v_aug_set")
    q_clear = sem("q_clear")
    q_clear_dve = sem("q_clear_dve")
    q_clear_act = sem("q_clear_act")
    x_t_in = sem("x_t_in")
    x_res_in = sem("x_res_in")
    x_res_sum = sem("x_res_sum")
    side_full = sem("side_full")
    side_free = sem("side_free")
    high_part = sem("high_part")
    rest_done = sem("rest_done")
    mid_part = sem("mid_part")
    split = sem("split")
    stacked = [sem(f"stacked{q}") for q in range(QUADS)]
    v_ready = sem("v_ready")
    max_full = sem("max_full")
    max_taken = sem("max_taken")
    neg_done = sem("neg_done")
    shift_step = sem("shift_step")
    shift_split = sem("shift_split")
    shift_in = sem("shift_in")
    exp_full = sem("exp_full")
    exp_done = sem("exp_done")
    masked = sem("masked")
    pv_done = sem("pv_done")
    o_taken = sem("o_taken")
    recip_done = sem("recip_done")
    ln_step = sem("ln_step")
    var_ready = sem("var_ready")
    rstd_done = sem("rstd_done")
    x1_ready = sem("x1_ready")
    x1_out = [sem(f"x1_out{half}") for half in range(2)]
    route_const = sem("route_const")
    rows_in = [sem(f"rows_in{half}") for half in range(2)]
    top_step = sem("top_step")
    diff_done = sem("diff_done")
    ex_done = sem("ex_done")
    gate_step = sem("gate_step")
    dest_step = sem("dest_step")
    hot_done = sem("hot_done")
    place_step = sem("place_step")
    row_ready = sem("row_ready")
    scattered = [sem(f"scattered{half}") for half in range(2)]
    tab_step = sem("tab_step")
    carry_done = sem("carry_done")
    padded = sem("padded")

    NCONST = 8

    CONSTS_IN = (const_in, 16 * NCONST)
    CHUNKS = [(c, which) for c in range(T // BANK) for which in range(2)]
    block = ctx.enter_context(nc.Block())

    @block.sync
    def _(sp):
        for dst, src in ((w_qkv, wqkvT), (rope, ropeT), (b_qk, bqk), (b_v, bv_rows), (w_p, wpT), (b_p, bp_rows),
                         (w_r, wr), (b_r, br_rows)):
            if dst is rope:
                sp.dma_start(x_t[:, :], xT[:, 0:T]).then_inc(x_t_in, 16)
            sp.dma_start(dst[:, :], src).then_inc(const_in, 16)

        def stack(b, q):
            first = isinstance(b, int) and b == 0
            if first:
                sp.wait_ge(q_clear, q + 1)
                sp.wait_ge(q_clear_act if q else q_clear_dve, max(q, 1))
            else:
                wait_apart(sp, CONSTS_IN, (split, 4 * b + 4), (exp_full, (4 * b + q - 3) * NEXP))
            rows = slice(GRP * q, GRP * (q + 1))
            for part in range(PARTS):
                if first:
                    sp.wait_ge((high_part, mid_part, split)[part], 4)
                for n in range(PARTS):
                    r = GRP * part + HD * n
                    sp.dma_start(q_st[q][r:r + HD, :, :], parts[rows, 0, part, :]).then_inc(stacked[q], 16)
                    r = GRP * n + HD * part
                    sp.dma_start(k_st[q][r:r + HD, :, :], parts[rows, 1, part, :]).then_inc(stacked[q], 16)

        def shift_rows(b, q, at):
            sp.wait_ge(side_free, at + 1)
            sp.dma_start(q_st[q][SHIFT_ROW:SHIFT_ROW + PARTS, :, :], shift_t[:, :]).then_inc(shift_in, 16)

        def store_x1(b, half):
            wait_apart(sp, CONSTS_IN, (x1_ready, 2 * b + half + 1))
            sp.dma_start(x1_dram[bass.ds(b * T + half * BANK, BANK), :].rearrange("(i p) c -> p i c", p=P),
                         x1[:, HT * half:HT * (half + 1), :]).then_inc(x1_out[half], 16)

        def load_rows(b, half):
            waits = [(x1_out[half], 16 * b + 16)]
            if not (isinstance(b, int) and b == 0):
                waits += [(scattered[half], ROWS_STEP * b)]
            wait_apart(sp, CONSTS_IN, *waits)
            for r in range(CHOICES):
                sp.dma_start(rows[:, half, r, :, 0:C],
                             x1_dram[bass.ds(b * T + half * BANK, BANK), :].rearrange("(i p) c -> p i c", p=P))\
                  .then_inc(rows_in[half], 16)

        def unit(b, q):
            if q == 0:
                stack(b, 3)
                if not absent(b, q, "xt0-"):
                    store_x1(b - 1, 0)
                    load_rows(b - 1, 0)
                    store_x1(b - 1, 1)
            if q == 1:
                wait_apart(sp, CONSTS_IN, (side_free, side_at(b, 0, "otr0") + 1))
                sp.dma_start(x_res[:, :, :], x[bass.ds(b * T, T), :].rearrange("(i p) c -> p i c", p=P))\
                  .then_inc(x_res_in, 16)
                if not absent(b, q, "q0+"):
                    wait_apart(sp, CONSTS_IN, (side_full, side_at(b, 0, "otr0")))
                    sp.dma_start(x_t[:, :], xT[:, bass.ds((b + 1) * T, T)]).then_inc(x_t_in, 16)
                if not absent(b, q, "rk1-"):
                    load_rows(b - 1, 1)
            if q == 2:
                if not (isinstance(b, int) and b == B - 1):
                    stack(b + 1, 1)
            if q == 3 and not (isinstance(b, int) and b == B - 1):
                stack(b + 1, 2)
            if not absent(b, q, "mt+"):
                shift_rows(b + (q + 1) // 4, (q + 1) % 4, side_at(b, q, "mt+"))
            if q == 1 and not absent(b, q, "q0+"):
                stack(b + 1, 0)

        stack(0, 0)
        stack(0, 1)
        shift_rows(0, 0, START.index("mt+"))
        stack(0, 2)
        for q in range(QUADS):
            unit(0, q)
        with sp.Fori(1, B - 1) as b:
            for q in range(QUADS):
                unit(b, q)
        for q in range(QUADS):
            unit(B - 1, q)
        store_x1(B - 1, 0)
        load_rows(B - 1, 0)
        store_x1(B - 1, 1)
        load_rows(B - 1, 1)
        sp.wait_ge(carry_done, 1)
        for e in range(E):
            row = sp.value_load(carry_i[0:1, e:e + 1], min_val=REGION * e, max_val=REGION * e + N)
            sp.dma_start(rows_dram[bass.ds(row, BLK), :].rearrange("(j p) c -> p j c", p=P), pad[:, :, :])\
              .then_inc(padded, 16)
        sp.dma_start(rows_dram[REGION * E:REGION * E + BLK, :].rearrange("(j p) c -> p j c", p=P), pad[:, :, :])\
          .then_inc(padded, 16)
        sp.wait_ge(padded, 16 * (E + 1))

    def vfill_at(b):
        if isinstance(b, int) and b == 0:
            return START.index("v1+")
        return side_at(b - 1, 3, "v1+")

    @block.gpsimd
    def _(pool):
        pool.memset(ident[:, :], 0.0).then_inc(const_set, 1)
        pool.memset(causal[:, :], 0.0).then_inc(const_set, 1)
        pool.memset(minus_half[:, :], -0.5).then_inc(const_set, 1)
        pool.memset(zero[:, :], 0.0).then_inc(const_set, 1)
        pool.wait_ge(const_set, 4)
        pool.affine_select(out=ident[:, :], in_=ident[:, :], compare_op=ALU.not_equal, fill=1.0, base=0,
                           pattern=[[-1, P]], channel_multiplier=1).then_inc(const_set, 1)
        pool.affine_select(out=causal[:, :], in_=causal[:, :], compare_op=ALU.is_ge, fill=MASKED, base=0,
                           pattern=[[-1, P]], channel_multiplier=1).then_inc(const_set, 1)
        pool.wait_ge(const_set, 6)
        pool.tensor_copy(ident_b[:, :], ident[:, :]).then_inc(const_set, 1)

        def rest_of(b, which, c):
            n = 4 * b + 2 * c + which
            cols = slice(BANK * c, BANK * (c + 1))
            pool.wait_ge(high_part, n + 1)
            pool.tensor_tensor(rest[:, which, cols], qk[:, which, cols], parts[:, which, 0, cols], ALU.subtract)\
                .then_inc(rest_done, 1)

        def low_part(b, which, c):
            n = 4 * b + 2 * c + which
            cols = slice(BANK * c, BANK * (c + 1))
            pool.wait_ge(mid_part, n + 1)
            pool.tensor_tensor(parts[:, which, 2, cols], rest[:, which, cols], parts[:, which, 1, cols],
                               ALU.subtract).then_inc(split, 1)

        def split_shift(u, u_parity):
            old = neg[:, u_parity, 0, :, :]
            waits = [(neg_done, u + 1)]
            if not (isinstance(u, int) and u == 0):
                waits += [(shift_in, 16 * u)]
            wait_apart(pool, CONSTS_IN, *waits)
            pool.tensor_copy(shift[:, 0, :, :], old).then_inc(shift_step, 1)
            pool.wait_ge(shift_step, 3 * u + 1)
            pool.tensor_tensor(neg_r[:, :, :], old, shift[:, 0, :, :], ALU.subtract)\
                .then_inc(shift_step, 1)
            wait_apart(pool, CONSTS_IN, (shift_step, 3 * u + 2))
            pool.tensor_copy(shift[:, 1, :, :], neg_r[:, :, :]).then_inc(shift_step, 1)
            pool.wait_ge(shift_step, 3 * u + 3)
            pool.tensor_tensor(shift[:, 2, :, :], neg_r[:, :, :], shift[:, 1, :, :], ALU.subtract)\
                .then_inc(shift_split, 1)

        def copy_v(b, q, at):
            first = isinstance(b, int) and b == 0
            wait_apart(pool, CONSTS_IN, (side_free, at + 1),
                       (v_aug_set, 2) if first else (pv_done, (4 * b + q - 3) * NG))
            pool.tensor_copy(v_aug[:, q, :, :, 0:HD],
                             v_st[:, :, GRP * q:GRP * (q + 1)].rearrange("p i (h d) -> p i h d", d=HD))\
                .then_inc(v_ready, 1)

        def mask_weights(u, g):
            c, j, q0, w, _, _ = GROUPS[g]
            wait_apart(pool, CONSTS_IN, (exp_done, u * NEXP + FILL0[g] + FILLS[g]))
            view = pt[:, g % PT_SLOTS, :, 0:P]
            pool.affine_select(out=view, in_=view, compare_op=ALU.is_ge, fill=0.0, base=0,
                               pattern=[[0, HQ], [1, P]], channel_multiplier=-1).then_inc(masked, 1)

        def inverse_std(b, half):
            pool.wait_ge(var_ready, 2 * b + half + 1)
            tiles = slice(HT * half, HT * (half + 1))
            pool.tensor_tensor(rstd[:, tiles], var_e[:, tiles], minus_half[:, tiles], ALU.pow).then_inc(rstd_done, 1)

        def scatter(b, columns):
            half = columns[0] // JR
            wait_apart(pool, CONSTS_IN, (row_ready, 2 * b + half + 1), (rows_in[half], 16 * CHOICES * (b + 1)))
            for column in columns:
                j = column % JR
                pool.indirect_dma_start(rows_dram[:, :],
                                        bass.IndirectOffsetOnAxis(ap=row_i[:, half, j:j + 1], axis=0),
                                        rows[:, half, j // HT, j % HT, :], None).then_inc(scattered[half], 16)

        def unit(b, q):
            u = 4 * b + q
            for g in range(NG):
                if g in DIAG:
                    mask_weights(u, g)
                if g == 7 and not absent(b, q, "mt+"):
                    split_shift(u + 1, (q + 1) % 2)
                if (q, g) in SCATTERS and not absent(b, 1, "rk1-"):
                    scatter(b - 1, SCATTERS[q, g])
                if q == 1 and g == 8 and not absent(b, q, "q0+"):
                    rest_of(b + 1, CHUNKS[3][1], CHUNKS[3][0])
                    low_part(b + 1, CHUNKS[3][1], CHUNKS[3][0])
                if g == 3:
                    if q == 0:
                        copy_v(b, 3, vfill_at(b))
                    if q == 1 and not absent(b, q, "q0+"):
                        for c, which in CHUNKS[:3]:
                            rest_of(b + 1, which, c)
                            low_part(b + 1, which, c)
                    if q == 2:
                        pool.wait_ge(x_res_in, 16 * b + 16)
                        pool.tensor_tensor(x_res[:, :, :], x_res[:, :, :],
                                           b_p[:, :].unsqueeze(1).to_broadcast([P, TILES, C]), ALU.add)\
                            .then_inc(x_res_sum, 1)
                    if q == 3 and not absent(b, q, "v0+"):
                        for p in range(3):
                            copy_v(b + 1, p, side_at(b, q, "v1+"))
                if (q, g) == INVERSE_STD[0]:
                    inverse_std(b, 0)
                if (q, g) == INVERSE_STD[1] and not absent(b, q, "y1-"):
                    inverse_std(b - 1, 1)

        pool.wait_ge(const_set, 7)
        for q in range(QUADS):
            pool.memset(k_st[q][SHIFT_ROW:P, :, :].bitcast(U32), 0x3F803F80).then_inc(q_clear, 1)
        pool.wait_ge(q_clear, QUADS)
        for c, which in CHUNKS:
            rest_of(0, which, c)
        pool.wait_ge(v_aug_set, 1)
        pool.memset(v_aug[:, :, :, :, HD:HD + 1], 1.0).then_inc(v_aug_set, 1)
        for q in range(3):
            copy_v(0, q, START.index("v1+"))
        split_shift(0, 0)
        pool.iota(iota_e[:, :], pattern=[[1, E]], base=0, channel_multiplier=0,
                  allow_small_or_imprecise_dtypes=True).then_inc(route_const, 1)
        pool.iota(dest[:, :].rearrange("p (r i) -> p r i", r=CHOICES), pattern=[[N, CHOICES], [P, HT]], base=0,
                  channel_multiplier=1, allow_small_or_imprecise_dtypes=True).then_inc(route_const, 1)
        pool.iota(carry[:, :], pattern=[[REGION, E]], base=0, channel_multiplier=0,
                  allow_small_or_imprecise_dtypes=True).then_inc(route_const, 1)
        pool.memset(ones[:, :], 1.0).then_inc(route_const, 1)
        pool.memset(hot[:, 0, :], 0.0).then_inc(route_const, 1)
        pool.iota(first_row[:, :], pattern=[[REGION, E]], base=0, channel_multiplier=0,
                  allow_small_or_imprecise_dtypes=True).then_inc(route_const, 1)
        pool.iota(steps_m[:, :], pattern=[[BLK, MOST]], base=0, channel_multiplier=0,
                  allow_small_or_imprecise_dtypes=True).then_inc(route_const, 1)
        pool.iota(block_no[:, :], pattern=[[1, NBLK]], base=0, channel_multiplier=0,
                  allow_small_or_imprecise_dtypes=True).then_inc(route_const, 1)
        pool.memset(pad[:, :, :], 0.0).then_inc(route_const, 1)
        pool.wait_ge(route_const, 9)
        pool.memset(pad[:, :, C + 1:C + 2], float(NOWHERE)).then_inc(route_const, 1)
        pool.affine_select(out=tri[:, :], in_=ones[:, :], compare_op=ALU.is_gt, fill=0.0, base=0,
                           pattern=[[1, P]], channel_multiplier=-1).then_inc(route_const, 1)
        for q in range(QUADS):
            unit(0, q)
        with pool.Fori(1, B - 1) as b:
            for q in range(QUADS):
                unit(b, q)
        for q in range(QUADS):
            unit(B - 1, q)
        inverse_std(B - 1, 1)
        scatter(B - 1, range(JR))
        scatter(B - 1, range(JR, 2 * JR))
        for half in range(2):
            pool.wait_ge(scattered[half], ROWS_STEP * B)

    @block.scalar
    def _(act):
        def exps(u, g):
            c, j, q0, w, _, per_bank = GROUPS[g]
            slot = g % PT_SLOTS
            for k in range(FILLS[g]):
                f = u * NEXP + FILL0[g] + k
                if k == 0 and not (isinstance(u, int) and u == 0 and g < PT_SLOTS):
                    act.wait_ge(pv_done, u * NG + g - PT_SLOTS + 1)
                act.wait_ge(exp_full, f + 1)
                act.activation(pt[:, slot, k * per_bank:(k + 1) * per_bank, 0:w],
                               ring_exp[(FILL0[g] + k) % RING_EXP][:, 0:per_bank * w].rearrange("p (h w) -> p h w", w=w),
                               ACT.Exp, scale=SCALE).then_inc(exp_done, 1)

        def take_o(u, c):
            act.wait_ge(pv_done, u * NG + LAST_OF_CHUNK[c] + 1)
            act.activation(o_t[:, c, :], o_bank[:, :], ACT.Copy).then_inc(o_taken, 1)

        def copy_out(dst, at):
            act.wait_ge(side_full, at + 1)
            act.activation(dst, side[:, :].rearrange("p (i t) -> p i t", t=P), ACT.Copy).then_inc(side_free, 1)

        def middle_part(b, c, which):
            cols = slice(BANK * c, BANK * (c + 1))
            act.wait_ge(rest_done, 4 * b + 2 * c + which + 1)
            act.activation(parts[:, which, 1, cols], rest[:, which, cols], ACT.Copy).then_inc(mid_part, 1)

        def side_job(job, at):
            if job[:3] == "ont":
                copy_out(on_t[:, :, :], at)
            if job[:2] == "xt":
                half = int(job[2])
                copy_out(x1_t[:, 4 * half:4 * half + 4, :], at)

        def gate_exp(b, half):
            act.wait_ge(diff_done, 2 * b + half + 1)
            act.activation(ex[:, :], diff[:, :], ACT.Exp).then_inc(ex_done, 1)

        def unit(b, q):
            u = 4 * b + q
            for g in range(NG):
                exps(u, g)
                if (q, g) in GATE_EXP and not absent(b, 1, "rk1-"):
                    gate_exp(b - 1, GATE_EXP.index((q, g)))
                if g == LAG - 1 and not (isinstance(b, int) and b == 0 and q == 0):
                    take_o(u - 1, 1)
                if g == LAST_OF_CHUNK[0] + LAG:
                    take_o(u, 0)
                for after, job in SIDE[q]:
                    if after == g and not absent(b, q, job):
                        side_job(job, side_at(b, q, job))
                if q == 1 and g in MIDDLE_PARTS and not absent(b, q, "q0+"):
                    middle_part(b + 1, *CHUNKS[MIDDLE_PARTS.index(g)])

        act.wait_ge(const_set, 4)
        for q in range(1, QUADS):
            for st in (q_st[q][:, :, :], k_st[q][0:SHIFT_ROW, :, :]):
                rows = st.shape[0]
                ins = act.activation(st.rearrange("p h t -> p (h t)").bitcast(F32),
                                     zero[0:rows, :].to_broadcast([rows, HQ * T // 2]), ACT.Copy)
            ins.then_inc(q_clear_act, 1)
            if q == 1:
                for c, which in CHUNKS:
                    middle_part(0, c, which)
        act.activation(v_aug[:, :, :, :, :].rearrange("p q i h d -> p (q i h d)"),
                       zero[:, :].to_broadcast([P, QUADS * TILES * HQ * GRP]), ACT.Copy).then_inc(v_aug_set, 1)
        for q in range(QUADS):
            unit(0, q)
        with act.Fori(1, B - 1) as b:
            for q in range(QUADS):
                unit(b, q)
        for q in range(QUADS):
            unit(B - 1, q)
        take_o(4 * B - 1, 1)
        for job in FLUSH:
            side_job(job, flush_at(job))
            if job == "y1-":
                gate_exp(B - 1, 0)
        gate_exp(B - 1, 1)

    @block.vector
    def _(dve):
        def reduce_fill(b, q, n):
            i, piece, h0, heads, k0, w = MAX_FILLS[n]
            u = 4 * b + q
            if n == 0 and not (isinstance(u, int) and u < 2):
                dve.wait_ge(shift_split, u - 1)
            dve.wait_ge(max_full, u * NMAX + n + 1)
            dve.tensor_reduce(neg[:, q % 2, piece, h0:h0 + heads, i],
                              ring_max[n % RING_MAX][:, 0:heads * w].rearrange("p (h w) -> p h w", w=w),
                              AX.X, ALU.max, negate=True).then_inc(max_taken, 1)
            if n == NMAX - 1:
                dve.wait_ge(max_taken, (u + 1) * NMAX)
                late = neg[:, q % 2, 0, :, TILES // 2:]
                dve.tensor_tensor(late, late, neg[:, q % 2, 1, :, TILES // 2:], ALU.min).then_inc(neg_done, 1)

        def side_job(b, q, job, at):
            name = job.rstrip("+-")
            dve.wait_ge(side_full, at + 1)
            if name in ("q0", "q1", "k0", "k1"):
                which, c = "qk".index(name[0]), int(name[1])
                if not (isinstance(b, int) and b == 0):
                    dve.wait_ge(split, 4 * b)
                    for p in range(QUADS):
                        dve.wait_ge(stacked[p], 16 * STACK_DMAS * b)
                cols = slice(BANK * c, BANK * (c + 1))
                dve.scalar_tensor_tensor(out=qk[:, which, cols], in0=side_bank(at)[:, :], scalar=b_qk[:, which:which + 1],
                                         in1=rope[:, cols], op0=ALU.add, op1=ALU.mult).then_inc(side_free, 1)
                dve.wait_ge(side_free, at + 1)
                dve.tensor_copy(parts[:, which, 0, cols], qk[:, which, cols]).then_inc(high_part, 1)
            elif name in ("v0", "v1"):
                c = int(name[1])
                if not (isinstance(b, int) and b == 0):
                    dve.wait_ge(v_ready, 4 * b)
                dve.tensor_tensor(v_st[:, 4 * c:4 * c + 4, :], side[:, :].rearrange("p (i c) -> p i c", c=C),
                                  b_v[:, :].unsqueeze(1).to_broadcast([P, 4, C]), ALU.add).then_inc(side_free, 1)
            elif name == "mt":
                u = 4 * b + q
                if not (isinstance(u, int) and u == 0):
                    dve.wait_ge(shift_in, 16 * u)
                dve.tensor_copy(shift_t[:, :], side_b[0:PARTS * HQ * TILES, 0:P]).then_inc(side_free, 1)
            elif name in ("otr0", "otr1"):
                c = int(name[3])
                view = side[:, :].rearrange("p (i h d) -> p i h d", h=HQ, d=GRP)
                dve.reciprocal(rden[:, :, :], view[:, :, :, HD]).then_inc(recip_done, 1)
                dve.wait_ge(recip_done, 2 * (4 * b + q) + c + 1)
                dve.tensor_tensor(
                    o_n[:, 4 * c:4 * c + 4, GRP * q:GRP * (q + 1)].rearrange("p i (h d) -> p i h d", d=HD),
                    view[:, :, :, 0:HD], rden[:, :, :].unsqueeze(3).to_broadcast([P, 4, HQ, HD]), ALU.mult)\
                    .then_inc(side_free, 1)
            elif name in ("y0", "y1"):
                half = int(name[1])
                step = 8 * (2 * b + half)
                dve.wait_ge(x_res_sum, b + 1)
                tiles = slice(4 * half, 4 * half + 4)
                dve.tensor_tensor(res[:, tiles, :], side[:, :].rearrange("p (i c) -> p i c", c=C),
                                  x_res[:, tiles, :], ALU.add).then_inc(side_free, 1)
                dve.wait_ge(side_free, at + 1)
                for i in range(4):
                    dve.bn_stats(stats[:, 4 * half + i, :], res[:, 4 * half + i, :]).then_inc(ln_step, 1)
                wait_apart(dve, CONSTS_IN, (ln_step, step + 4))
                for i in range(4):
                    dve.bn_aggr(mv[:, 4 * half + i, :], stats[:, 4 * half + i, :]).then_inc(ln_step, 1)
                dve.wait_ge(ln_step, step + 8)
                dve.tensor_scalar(var_e[:, tiles], mv[:, tiles, 1], EPS, None, ALU.add).then_inc(var_ready, 1)

        def normalise(b, half):
            dve.wait_ge(rstd_done, 2 * b + half + 1)
            if not (isinstance(b, int) and b == 0):
                dve.wait_ge(x1_out[half], 16 * b)
            for i in range(4 * half, 4 * half + 4):
                ins = dve.tensor_scalar(x1[:, i, :], res[:, i, :], mv[:, i, 0:1], rstd[:, i:i + 1],
                                        ALU.subtract, ALU.mult)
            ins.then_inc(x1_ready, 1)

        def take_logits(b, at):
            dve.wait_ge(side_full, at + 1)
            dve.tensor_tensor(logits[:, :, :],
                              side[:, 0:HT * E].rearrange("p (i e) -> p i e", e=E),
                              b_r[:, :].unsqueeze(1).to_broadcast([P, HT, E]), ALU.add).then_inc(side_free, 1)

        def top_two(b, half):
            n = 2 * b + half
            dve.wait_ge(route_const, ROUTE_CONSTS)
            job = f"rl{half}-"
            at = flush_at(job) if isinstance(b, int) and b == B - 1 else side_at(b + 1, half, job)
            dve.wait_ge(side_free, at + 1)
            for i in range(HT):
                dve.max(top[:, i, :], logits[:, i, :]).then_inc(top_step, 1)
            dve.wait_ge(top_step, 2 * HT * n + HT)
            dve.tensor_tensor(diff[:, :], top[:, :, 1], top[:, :, 0], ALU.subtract).then_inc(diff_done, 1)

        def one_hots(b, half):
            n = 2 * b + half
            for i in range(HT):
                dve.max_index(topi[:, i, :], top[:, i, :], logits[:, i, :]).then_inc(top_step, 1)
            dve.wait_ge(top_step, 2 * HT * (n + 1))
            dve.tensor_copy(topf[:, :].rearrange("p (r i) -> p i r", r=CHOICES), topi[:, :, 0:CHOICES])\
               .then_inc(gate_step, 1)
            dve.wait_ge(gate_step, 5 * n + 1)
            dve.tensor_tensor(hot[:, 1:, :], topf[:, :].unsqueeze(2).to_broadcast([P, JR, E]),
                              iota_e[:, :].unsqueeze(1).to_broadcast([P, JR, E]), ALU.is_equal).then_inc(hot_done, 1)

        def gates(b, half):
            n = 2 * b + half
            dve.wait_ge(ex_done, n + 1)
            dve.tensor_scalar(den[:, :], ex[:, :], 1.0, None, ALU.add).then_inc(gate_step, 1)
            if not (isinstance(b, int) and b == 0):
                dve.wait_ge(scattered[half], ROWS_STEP * b)
            if not (isinstance(n, int) and n == 0):
                dve.wait_ge(dest_step, n)
            dve.wait_ge(gate_step, 5 * n + 2)
            dve.reciprocal(rows[:, half, 0, :, C], den[:, :]).then_inc(gate_step, 1)
            dve.wait_ge(gate_step, 5 * n + 3)
            dve.tensor_tensor(rows[:, half, 1, :, C], rows[:, half, 0, :, C], ex[:, :], ALU.mult).then_inc(gate_step, 1)
            dve.tensor_copy(rows[:, half, :, :, C + 1], dest[:, :].rearrange("p (r i) -> p r i", r=CHOICES))\
               .then_inc(gate_step, 1)

        def row_numbers(b, half, at):
            n = 2 * b + half
            dve.wait_ge(side_full, at + 1)
            dve.tensor_tensor(place[:, :, :], side[:, 0:JR * E].rearrange("p (j e) -> p j e", e=E),
                              carry[:, :].unsqueeze(1).to_broadcast([P, JR, E]), ALU.add).then_inc(place_step, 1)
            dve.wait_ge(place_step, 3 * n + 1)
            dve.tensor_tensor(carry[:, :], carry[:, :], side[:, JR * E:(JR + 1) * E], ALU.add).then_inc(side_free, 1)
            dve.tensor_tensor(place[:, :, :], place[:, :, :], hot[:, 1:, :], ALU.mult).then_inc(place_step, 1)
            dve.wait_ge(place_step, 3 * n + 2)
            dve.tensor_reduce(row_f[:, :], place[:, :, :], AX.X, ALU.add).then_inc(place_step, 1)
            dve.wait_ge(gate_step, 5 * n + 5)
            dve.tensor_scalar(dest[:, :], dest[:, :], float(BANK), None, ALU.add).then_inc(dest_step, 1)
            dve.wait_ge(place_step, 3 * n + 3)
            dve.tensor_copy(row_i[:, half, :], row_f[:, :]).then_inc(row_ready, 1)

        def block_tables():
            dve.wait_ge(side_free, len(SIDE_ORDER))
            dve.tensor_tensor(count[:, :], carry[:, :], first_row[:, :], ALU.subtract).then_inc(tab_step, 1)
            dve.tensor_copy(carry_i[:, :], carry[:, :]).then_inc(carry_done, 1)
            dve.wait_ge(tab_step, 1)
            dve.tensor_tensor(over[:, :, :], count[:, :].unsqueeze(2).to_broadcast([P, E, MOST]),
                              steps_m[:, :].unsqueeze(1).to_broadcast([P, E, MOST]), ALU.is_gt).then_inc(tab_step, 1)
            dve.wait_ge(tab_step, 2)
            dve.tensor_reduce(blocks[:, :], over[:, :, :], AX.X, ALU.add).then_inc(tab_step, 1)
            dve.wait_ge(tab_step, 3)
            dve.tensor_copy(ends[:, 0, :], blocks[:, :]).then_inc(tab_step, 1)
            at = 4
            for n in range(3):
                src, dst, by = n % 2, 1 - n % 2, 1 << n
                dve.wait_ge(tab_step, at)
                dve.tensor_copy(ends[:, dst, 0:by], ends[:, src, 0:by]).then_inc(tab_step, 1)
                dve.tensor_tensor(ends[:, dst, by:], ends[:, src, by:], ends[:, src, :E - by], ALU.add)\
                   .then_inc(tab_step, 1)
                at += 2
            dve.wait_ge(tab_step, at)
            blocks_shape = [P, NBLK, E]
            dve.tensor_tensor(past[:, :, :], block_no[:, :].unsqueeze(2).to_broadcast(blocks_shape),
                              ends[:, 1, :].unsqueeze(1).to_broadcast(blocks_shape), ALU.is_ge).then_inc(tab_step, 1)
            dve.wait_ge(tab_step, at + 1)
            dve.tensor_tensor(past_end[:, :, :], past[:, :, :], ends[:, 1, :].unsqueeze(1).to_broadcast(blocks_shape),
                              ALU.mult).then_inc(tab_step, 1)
            dve.tensor_reduce(expert_f[:, :], past[:, :, :], AX.X, ALU.add).then_inc(tab_step, 1)
            dve.wait_ge(tab_step, at + 3)
            dve.tensor_reduce(start_f[:, :], past_end[:, :, :], AX.X, ALU.max).then_inc(tab_step, 1)
            dve.tensor_scalar(used[:, :], expert_f[:, :], float(E), float(BLK), ALU.is_lt, ALU.mult).then_inc(tab_step, 1)
            dve.tensor_scalar(table[:, 0, :], expert_f[:, :], float(E - 1), float(P), ALU.min, ALU.mult)\
               .then_inc(tab_step, 1)
            dve.wait_ge(tab_step, at + 6)
            dve.tensor_tensor(nth[:, :], block_no[:, :], start_f[:, :], ALU.subtract).then_inc(tab_step, 1)
            dve.wait_ge(tab_step, at + 7)
            dve.tensor_tensor(nth[:, :], nth[:, :], used[:, :], ALU.mult).then_inc(tab_step, 1)
            dve.tensor_scalar(row0_f[:, :], expert_f[:, :], float(REGION), None, ALU.mult).then_inc(tab_step, 1)
            dve.wait_ge(tab_step, at + 9)
            dve.tensor_tensor(table[:, 1, :], row0_f[:, :], nth[:, :], ALU.add).then_inc(tab_step, 1)

        def run_side(b, q, job, at):
            if job[:2] == "rk":
                row_numbers(b - 1, int(job[2]), at)
            elif job == "otr1-":
                pb, pq = (b - 1, 3) if q == 0 else (b, q - 1)
                side_job(pb, pq, job, at)
            elif job == "y1-":
                side_job(b - 1, q, job, at)
            elif job[:2] == "rl":
                take_logits(b - 1, at)
            elif job in ("otr0", "y0"):
                side_job(b, q, job, at)
            elif job == "mt+":
                side_job(b + (q + 1) // 4, (q + 1) % 4, job, at)
            elif job[0] in "qkv":
                side_job(b + 1, q, job, at)

        def unit(b, q):
            u = 4 * b + q
            for g in range(NG):
                for k in range(FILLS[g]):
                    fill = max_fill_beside(b, q, FILL0[g] + k)
                    if fill:
                        reduce_fill(*fill)
                if not absent(b, 1, "rk1-"):
                    for half in range(2):
                        if (q, g) == NORMALISE[half]:
                            normalise(b - 1, half)
                        if (q, g) == TOP_TWO[half]:
                            top_two(b - 1, half)
                        if (q, g) == ONE_HOTS[half]:
                            one_hots(b - 1, half)
                        if (q, g) == GATES[half]:
                            gates(b - 1, half)
                for after, job in SIDE[q]:
                    if after == g and not absent(b, q, job):
                        run_side(b, q, job, side_at(b, q, job))

        dve.memset(q_st[0][:, :, :].bitcast(U32), 0)
        dve.memset(k_st[0][0:SHIFT_ROW, :, :].bitcast(U32), 0).then_inc(q_clear_dve, 1)
        dve.wait_ge(const_in, 16 * NCONST)
        for job in START[:4]:
            side_job(0, 0, job, START.index(job))
        for n, (c, which) in enumerate(CHUNKS):
            cols = slice(BANK * c, BANK * (c + 1))
            dve.wait_ge(mid_part, n + 1)
            dve.tensor_tensor(parts[:, which, 2, cols], rest[:, which, cols], parts[:, which, 1, cols],
                              ALU.subtract).then_inc(split, 1)
        for job in START[4:-1]:
            side_job(0, 0, job, START.index(job))
        for n in range(NMAX):
            reduce_fill(0, 0, n)
        for n in range(AHEAD):
            if n == MT_AFTER:
                side_job(0, 0, "mt+", START.index("mt+"))
            reduce_fill(0, 1, n)
        for q in range(QUADS):
            unit(0, q)
        with dve.Fori(1, B - 1) as b:
            for q in range(QUADS):
                unit(b, q)
        for q in range(QUADS):
            unit(B - 1, q)
        for job in FLUSH:
            if job == "xt0-":
                normalise(B - 1, 0)
            run_side(B, 0, job, flush_at(job))
            if job == "y1-":
                top_two(B - 1, 0)
                one_hots(B - 1, 0)
                normalise(B - 1, 1)
                gates(B - 1, 0)
            if job == "rl1-":
                top_two(B - 1, 1)
                one_hots(B - 1, 1)
                gates(B - 1, 1)
        block_tables()

    @block.tensor
    def _(pe):
        def fill_max(b, q, n):
            i, piece, h0, heads, k0, w = MAX_FILLS[n]
            u = 4 * b + q
            if n == 0:
                pe.wait_ge(stacked[q], 16 * STACK_DMAS * (b + 1))
            if not (isinstance(u, int) and u == 0 and n < RING_MAX):
                pe.wait_ge(max_taken, taken_before(u, n, RING_MAX))
            diag = k0 + w == P * (i + 1)
            for h in range(heads):
                out = ring_max[n % RING_MAX][:, h * w:(h + 1) * w]
                last = pe.matmul(out, q_st[q][0:SHIFT_ROW, h0 + h, P * i:P * (i + 1)],
                                 k_st[q][0:SHIFT_ROW, h0 + h, k0:k0 + w], start=True, stop=not diag)
                if diag:
                    last = pe.matmul(out[:, w - P:w], ident_b[:, :], causal[:, :], start=False, stop=True)
            last.then_inc(max_full, 1)

        def fill_exp(u, q, g, k):
            c, j, q0, w, _, per_bank = GROUPS[g]
            s = FILL0[g] + k
            if s == 0:
                pe.wait_ge(shift_in, 16 * (u + 1))
            if not (isinstance(u, int) and u == 0 and s < RING_EXP):
                pe.wait_ge(exp_done, taken_before(u, s, RING_EXP))
            for h in range(per_bank):
                last = pe.matmul(ring_exp[s % RING_EXP][:, h * w:(h + 1) * w],
                                 k_st[q][0:SHIFT_ROW + PARTS, k * per_bank + h, P * j:P * (j + 1)],
                                 q_st[q][0:SHIFT_ROW + PARTS, k * per_bank + h, q0:q0 + w], start=True, stop=True)
            last.then_inc(exp_full, 1)

        def values(u, q, g):
            c, j, q0, w, is_diag, _ = GROUPS[g]
            if g == 0:
                pe.wait_ge(v_ready, u + 1)
            if j == 0 and not (isinstance(u, int) and u == 0 and c == 0):
                pe.wait_ge(o_taken, 2 * u + c)
            pe.wait_ge(exp_done, u * NEXP + FILL0[g] + FILLS[g])
            if is_diag:
                pe.wait_ge(masked, u * NDIAG + DIAG.index(g) + 1)
            for h in range(HQ):
                last = pe.matmul(o_bank[GRP * h:GRP * (h + 1), BANK - w:BANK], v_aug[:, q, j, h, :],
                                 pt[:, g % PT_SLOTS, h, 0:w], start=j == 0, stop=g == LAST_OF_CHUNK[c])
            last.then_inc(pv_done, 1)

        def side_job(b, q, job, at):
            name = job.rstrip("+-")
            if not (isinstance(at, int) and at <= len(start_banks)):
                pe.wait_ge(side_free, at)
            if name in ("q0", "q1", "k0", "k1"):
                which, c = "qk".index(name[0]), int(name[1])
                pe.wait_ge(x_t_in, 16 * b + 16)
                last = pe.matmul(side_bank(at)[:, :], w_qkv[:, C * which:C * (which + 1)], x_t[:, BANK * c:BANK * (c + 1)],
                                 start=True, stop=True)
            elif name in ("v0", "v1"):
                for i in range(4):
                    t0 = BANK * int(name[1]) + P * i
                    last = pe.matmul(side[:, C * i:C * (i + 1)], x_t[:, t0:t0 + P], w_qkv[:, 2 * C:3 * C],
                                     start=True, stop=True)
            elif name == "mt":
                pe.wait_ge(shift_split, 4 * b + q + 1)
                last = pe.transpose(side_b[0:PARTS * HQ * TILES, 0:P],
                                    shift[:, :, :, :].rearrange("p a h i -> p (a h i)"), ident_b[:, :])
            elif name in ("otr0", "otr1"):
                c = int(name[3])
                pe.wait_ge(o_taken, 2 * (4 * b + q) + c + 1)
                for i in range(4):
                    last = pe.transpose(side[:, P * i:P * (i + 1)], o_t[:, c, P * i:P * (i + 1)], ident[:, :])
            elif name in ("ont0", "ont1"):
                for i in range(4):
                    last = pe.transpose(side[:, P * i:P * (i + 1)], o_n[:, 4 * int(name[3]) + i, :], ident[:, :])
            elif name in ("y0", "y1"):
                for i in range(4):
                    last = pe.matmul(side[:, C * i:C * (i + 1)], on_t[:, i, :], w_p[:, :], start=True, stop=True)
            elif name in ("xt0", "xt1"):
                half = int(name[2])
                pe.wait_ge(x1_ready, 2 * b + half + 1)
                for i in range(4):
                    last = pe.transpose(side[:, P * i:P * (i + 1)], x1[:, 4 * half + i, :], ident[:, :])
            elif name in ("rl0", "rl1"):
                for i in range(HT):
                    last = pe.matmul(side[:, E * i:E * (i + 1)], x1_t[:, HT * int(name[2]) + i, :], w_r[:, :],
                                     start=True, stop=True)
            elif name in ("rk0", "rk1"):
                pe.wait_ge(route_const, ROUTE_CONSTS)
                pe.wait_ge(hot_done, 2 * b + int(name[2]) + 1)
                pe.matmul(side[:, 0:(JR + 1) * E], ones[:, :], hot[:, :, :].rearrange("p j e -> p (j e)"),
                          start=True, stop=False)
                for n in range(2, JR + 1):
                    pe.matmul(side[:, n * E:(JR + 1) * E], ones[:, :],
                              hot[:, 1:JR + 2 - n, :].rearrange("p j e -> p (j e)"), start=False, stop=False)
                last = pe.matmul(side[:, 0:JR * E], tri[:, :], hot[:, 1:, :].rearrange("p j e -> p (j e)"),
                                 start=False, stop=True)
            last.then_inc(side_full, 1)

        def run_side(b, q, job, at):
            if job == "otr1-":
                u = 4 * b + q
                if q == 0:
                    side_job(b - 1, 3, job, at)
                else:
                    side_job(b, q - 1, job, at)
            elif job == "mt+":
                side_job(b + (q + 1) // 4, (q + 1) % 4, job, at)
            elif job.endswith("+"):
                side_job(b + 1, q, job, at)
            elif job.endswith("-"):
                side_job(b - 1, q, job, at)
            else:
                side_job(b, q, job, at)

        def unit(b, q, b_max):
            u = 4 * b + q
            for g in range(NG):
                for k in range(FILLS[g]):
                    fill_exp(u, q, g, k)
                    fill = max_fill_beside(b_max, q, FILL0[g] + k)
                    if fill:
                        fill_max(*fill)
                    if k == min(VALUES_AFTER, FILLS[g] - 1):
                        if g >= LAG:
                            values(u, q, g - LAG)
                        elif not (isinstance(b, int) and b == 0 and q == 0):
                            values(u - 1, (q - 1) % 4, NG - LAG + g)
                for after, job in SIDE[q]:
                    if after == g and not absent(b, q, job):
                        run_side(b, q, job, side_at(b, q, job))

        pe.wait_ge(const_in, 16 * NCONST)
        pe.wait_ge(const_set, 7)
        for job in START[:-1]:
            side_job(0, 0, job, START.index(job))
        for n in range(NMAX):
            fill_max(0, 0, n)
        for n in range(AHEAD):
            if n == MT_AFTER + RING_MAX:
                side_job(0, 0, "mt+", START.index("mt+"))
            fill_max(0, 1, n)
        for q in range(QUADS):
            unit(0, q, 0)
        with pe.Fori(1, B - 1) as b:
            b_max = own_copy(pe, b)
            for q in range(QUADS):
                unit(b, q, b_max)
        for q in range(QUADS):
            unit(B - 1, q, B - 1)
        for g in range(NG - LAG, NG):
            values(4 * B - 1, 3, g)
        for job in FLUSH:
            run_side(B, 0, job, flush_at(job))


def experts(nc, ctx, x1_dram, rows_dram, y_dram, table, w_all, out):

    def sb(name, shape, dt):
        return ctx.enter_context(nc.sbuf_tensor(name, shape, dt))

    def ps(name, shape, dt):
        return ctx.enter_context(nc.psum_tensor(name, shape, dt))

    def sem(name):
        return ctx.enter_context(nc.semaphore(name))

    SLOTS = 8
    CT = BANK // P
    NC = NT // CT
    CHUNK_SLOTS = 4
    GROUPS_OF_BLOCKS = NBLK // SLOTS
    LAST = NBLK % SLOTS
    ident = sb("ident2", [P, P], F32)
    w = sb("w", [P, SLOTS, WROW], F32)
    xin = sb("xin", [P, SLOTS, BT, ROW], F32)
    dest_i = sb("dest_i", [P, SLOTS, BT], U32)
    xt = sb("xt", [P, 2, BLK], F32)
    hid = sb("hid", [P, 2, HC, BLK], F32)
    y_sum = sb("y_sum", [P, 2, BT, C], F32)
    y_gated = sb("y_gated", [P, SLOTS, BT, C], F32)
    x_fin = sb("x_fin", [P, NT, C], F32)
    y_fin = sb("y_fin", [P, CHOICES, NT, C], F32)
    y_pair = sb("y_pair", [P, CHUNK_SLOTS, CT, C], F32)
    acc = sb("acc", [P, CHUNK_SLOTS, CT, C], F32)
    stats = sb("stats2", [P, CHUNK_SLOTS, CT, 6], F32)
    mv = sb("mv2", [P, CHUNK_SLOTS, CT, 2], F32)
    var_e = sb("var_e2", [P, CHUNK_SLOTS, CT], F32)
    rstd = sb("rstd2", [P, CHUNK_SLOTS, CT], F32)
    shift = sb("shift2", [P, CHUNK_SLOTS, CT], F32)
    minus_half = sb("minus_half2", [P, CT], F32)
    y_out = sb("y_out", [P, CHUNK_SLOTS, CT, C], F32)

    hp = [ps(f"hp{i}", [P, BANK], F32) for i in range(4)]
    yp = [ps(f"yp{i}", [P, BANK], F32) for i in range(2)]
    tp = [ps(f"tp{i}", [P, BANK], F32) for i in range(2)]

    const_set = sem("const_set2")
    w_in = [sem(f"w_in{s}") for s in range(SLOTS)]
    rows_in = [sem(f"block_in{s}") for s in range(SLOTS)]
    x_turned = sem("x_turned")
    xt_done = sem("xt_done")
    hp_full = sem("hp_full")
    hid_done = sem("hid_done")
    yp_full = sem("yp_full")
    y_summed = sem("y_summed")
    dest_done = sem("dest_done")
    y_ready = sem("y_ready")
    y_written = [sem(f"y_written{s}") for s in range(SLOTS)]
    x_in = sem("x_in")
    y_in = [sem(f"y_in{c}") for c in range(NC)]
    pair_done = sem("pair_done")
    acc_done = sem("acc_done")
    ln_step = sem("ln_step2")
    var_ready = sem("var_ready2")
    rstd_done = sem("rstd_done2")
    shift_done = sem("shift_done")
    out_ready = sem("out_ready")
    out_stored = [sem(f"out_stored{s}") for s in range(CHUNK_SLOTS)]

    block = ctx.enter_context(nc.Block())

    def load_results(eng, r):
        for s in range(SLOTS):
            eng.wait_ge(y_written[s], 16 * BT * (GROUPS_OF_BLOCKS + (s < LAST)))
        for c in range(NC):
            rows = slice(N * r + BANK * c, N * r + BANK * (c + 1))
            eng.dma_start(y_fin[:, r, CT * c:CT * (c + 1), :], y_dram[rows, :].rearrange("(i p) c -> p i c", p=P))\
               .then_inc(y_in[c], 16)

    @block.sync
    def _(sp):
        def load(i, s):
            row = sp.value_load(table[0:1, 1, bass.ds(i, 1)], min_val=0, max_val=REGION * E)
            sp.dma_start(xin[:, s, :, :], rows_dram[bass.ds(row, BLK), :].rearrange("(j p) c -> p j c", p=P))\
              .then_inc(rows_in[s], 16)
            wrow = sp.value_load(table[0:1, 0, bass.ds(i, 1)], min_val=0, max_val=P * (E - 1))
            sp.dma_start(w[:, s, :], w_all[bass.ds(wrow, P), :]).then_inc(w_in[s], 16)

        for s in range(SLOTS):
            load(s, s)
        def refill(g, slots):
            for s in range(slots):
                sp.wait_ge(y_ready, SLOTS * (g - 1) + s + 1)
                load(SLOTS * g + s, s)

        with sp.Fori(1, GROUPS_OF_BLOCKS) as g:
            refill(g, SLOTS)
        refill(GROUPS_OF_BLOCKS, LAST)

        sp.dma_start(x_fin[:, :, :], x1_dram.rearrange("(i p) c -> p i c", p=P)).then_inc(x_in, 16)
        load_results(sp, 0)
        for c in range(NC):
            s = c % CHUNK_SLOTS
            sp.wait_ge(out_ready, CT * (c + 1))
            sp.dma_start(out[BANK * c:BANK * (c + 1), :].rearrange("(i p) c -> p i c", p=P), y_out[:, s, :, :])\
              .then_inc(out_stored[s], 16)
        for s in range(CHUNK_SLOTS):
            sp.wait_ge(out_stored[s], 16 * (NC // CHUNK_SLOTS))

    @block.gpsimd
    def _(pool):
        pool.memset(minus_half[:, :], -0.5).then_inc(const_set, 1)
        pool.memset(ident[:, :], 0.0).then_inc(const_set, 1)
        pool.wait_ge(const_set, 2)
        pool.affine_select(out=ident[:, :], in_=ident[:, :], compare_op=ALU.not_equal, fill=1.0, base=0,
                           pattern=[[-1, P]], channel_multiplier=1).then_inc(const_set, 1)

        def scatter(g, slots):
            for s in range(slots):
                wait_apart(pool, (const_set, 3), (y_ready, SLOTS * g + s + 1))
                for j in range(BT):
                    pool.indirect_dma_start(y_dram[:, :], bass.IndirectOffsetOnAxis(ap=dest_i[:, s, j:j + 1], axis=0),
                                            y_gated[:, s, j, :], None,
                                            bounds_check=NOWHERE - 1, oob_is_err=False).then_inc(y_written[s], 16)

        with pool.Fori(0, GROUPS_OF_BLOCKS) as g:
            scatter(g, SLOTS)
        scatter(GROUPS_OF_BLOCKS, LAST)

        def chunk(c, s):
            pool.wait_ge(y_in[c], 16 * CHOICES)
            if c >= CHUNK_SLOTS:
                pool.wait_ge(acc_done, c - CHUNK_SLOTS + 1)
            tiles = slice(CT * c, CT * (c + 1))
            pool.tensor_tensor(y_pair[:, s, :, :], y_fin[:, 0, tiles, :], y_fin[:, 1, tiles, :], ALU.add)\
                .then_inc(pair_done, 1)

        def inverse_std(c, s):
            pool.wait_ge(var_ready, c + 1)
            pool.tensor_tensor(rstd[:, s, :], var_e[:, s, :], minus_half[:, :], ALU.pow).then_inc(rstd_done, 1)

        for c in range(NC):
            chunk(c, c % CHUNK_SLOTS)
            if c >= 1:
                inverse_std(c - 1, (c - 1) % CHUNK_SLOTS)
        inverse_std(NC - 1, (NC - 1) % CHUNK_SLOTS)

    @block.scalar
    def _(act):
        def take_x(i, s):
            act.wait_ge(x_turned, i + 1)
            act.activation(xt[:, s % 2, :], tp[s % 2][:, 0:BLK], ACT.Copy).then_inc(xt_done, 1)

        def take_hidden(i, s):
            for k in range(HC):
                if k % 2 == 0:
                    act.wait_ge(hp_full, 2 * i + k // 2 + 1)
                act.activation(hid[:, s % 2, k, :], hp[2 * (s % 2) + k // 2][:, BLK * (k % 2):BLK * (k % 2 + 1)],
                               ACT.Relu, bias=w[:, s, H + HC * C + k:H + HC * C + k + 1]).then_inc(hid_done, 1)

        take_x(0, 0)
        def group(g, slots, more):
            for s in range(slots):
                i = SLOTS * g + s
                if more or s < slots - 1:
                    take_x(i + 1, s + 1)
                take_hidden(i, s)

        with act.Fori(0, GROUPS_OF_BLOCKS) as g:
            group(g, SLOTS, True)
        group(GROUPS_OF_BLOCKS, LAST, False)
        load_results(act, 1)

        for c in range(NC):
            s = c % CHUNK_SLOTS
            act.wait_ge(shift_done, c + 1)
            if c >= CHUNK_SLOTS:
                act.wait_ge(out_stored[s], 16 * (c // CHUNK_SLOTS))
            for k in range(CT):
                act.activation(y_out[:, s, k, :], acc[:, s, k, :], ACT.Identity, bias=shift[:, s, k:k + 1],
                               scale=rstd[:, s, k:k + 1]).then_inc(out_ready, 1)

    @block.vector
    def _(dve):
        dve.wait_ge(const_set, 3)
        def finish(g, i, s):
            if not (isinstance(g, int) and g == 0):
                dve.wait_ge(y_written[s], 16 * BT * g)
            dve.wait_ge(rows_in[s], 16 * (g + 1))
            dve.tensor_copy(dest_i[:, s, :], xin[:, s, :, C + 1]).then_inc(dest_done, 1)
            dve.wait_ge(yp_full, i + 1)
            dve.tensor_tensor(y_sum[:, s % 2, :, :], yp[s % 2][:, 0:BT * C].rearrange("p (j c) -> p j c", c=C),
                              w[:, s, H + HC * C + HC:].unsqueeze(1).to_broadcast([P, BT, C]), ALU.add)\
               .then_inc(y_summed, 1)
            dve.wait_ge(y_summed, i + 1)
            dve.wait_ge(dest_done, i + 1)
            dve.tensor_tensor(y_gated[:, s, :, :], y_sum[:, s % 2, :, :],
                              xin[:, s, :, C:C + 1].to_broadcast([P, BT, C]), ALU.mult).then_inc(y_ready, 1)

        for s in range(SLOTS):
            finish(0, s, s)
        with dve.Fori(1, GROUPS_OF_BLOCKS) as g:
            for s in range(SLOTS):
                finish(g, SLOTS * g + s, s)
        for s in range(LAST):
            finish(GROUPS_OF_BLOCKS, SLOTS * GROUPS_OF_BLOCKS + s, s)

        def statistics(c, s):
            dve.wait_ge(pair_done, c + 1)
            if c >= CHUNK_SLOTS:
                dve.wait_ge(out_ready, CT * (c - CHUNK_SLOTS + 1))
            dve.tensor_tensor(acc[:, s, :, :], y_pair[:, s, :, :], x_fin[:, CT * c:CT * (c + 1), :], ALU.add)\
               .then_inc(acc_done, 1)
            dve.wait_ge(acc_done, c + 1)
            for k in range(CT):
                dve.bn_stats(stats[:, s, k, :], acc[:, s, k, :]).then_inc(ln_step, 1)
            dve.wait_ge(ln_step, 8 * c + 4)
            for k in range(CT):
                dve.bn_aggr(mv[:, s, k, :], stats[:, s, k, :]).then_inc(ln_step, 1)
            dve.wait_ge(ln_step, 8 * c + 8)
            dve.tensor_scalar(var_e[:, s, :], mv[:, s, :, 1], EPS, None, ALU.add).then_inc(var_ready, 1)

        def shifts(c, s):
            dve.wait_ge(rstd_done, c + 1)
            dve.scalar_tensor_tensor(out=shift[:, s, :], in0=mv[:, s, :, 0], scalar=-1.0, in1=rstd[:, s, :],
                                     op0=ALU.mult, op1=ALU.mult).then_inc(shift_done, 1)

        dve.wait_ge(x_in, 16)
        for c in range(NC):
            statistics(c, c % CHUNK_SLOTS)
            if c >= 1:
                shifts(c - 1, (c - 1) % CHUNK_SLOTS)
        shifts(NC - 1, (NC - 1) % CHUNK_SLOTS)

    @block.tensor
    def _(pe):
        def turn(g, i, s):
            pe.wait_ge(rows_in[s], 16 * (g + 1))
            for j in range(BT):
                ins = pe.transpose(tp[s % 2][:, P * j:P * (j + 1)], xin[:, s, j, 0:C], ident[:, :])
            ins.then_inc(x_turned, 1)

        def up(g, i, s):
            pe.wait_ge(w_in[s], 16 * (g + 1))
            pe.wait_ge(xt_done, i + 1)
            if not (isinstance(i, int) and i < 2):
                pe.wait_ge(hid_done, HC * (i - 1))
            for k in range(HC):
                ins = pe.matmul(hp[2 * (s % 2) + k // 2][:, BLK * (k % 2):BLK * (k % 2 + 1)],
                                w[:, s, P * k:P * (k + 1)], xt[:, s % 2, :], start=True, stop=True)
                if k % 2:
                    ins.then_inc(hp_full, 1)

        def down(i, s):
            pe.wait_ge(hid_done, HC * (i + 1))
            if not (isinstance(i, int) and i < 2):
                pe.wait_ge(y_summed, i - 1)
            for j in range(BT):
                for k in range(HC):
                    ins = pe.matmul(yp[s % 2][:, C * j:C * (j + 1)], hid[:, s % 2, k, P * j:P * (j + 1)],
                                    w[:, s, H + C * k:H + C * (k + 1)], start=k == 0, stop=k == HC - 1)
            ins.then_inc(yp_full, 1)

        def step(g, s, more=True):
            i = SLOTS * g + s
            if more:
                turn(g + (s + 1) // SLOTS, i + 1, (s + 1) % SLOTS)
            up(g, i, s)
            if not (isinstance(i, int) and i == 0):
                down(i - 1, (s - 1) % SLOTS)

        pe.wait_ge(const_set, 3)
        turn(0, 0, 0)
        for s in range(SLOTS):
            step(0, s)
        with pe.Fori(1, GROUPS_OF_BLOCKS) as g:
            for s in range(SLOTS):
                step(g, s)
        for s in range(LAST):
            step(GROUPS_OF_BLOCKS, s, s < LAST - 1)
        down(NBLK - 1, LAST - 1)


def program(nc, x, xT, ropeT, wqkvT, bqk, bv_rows, wpT, bp_rows, wr, br_rows, w_all, out):
    x1_dram = nc.dram_tensor("x1_dram", (N, C), F32, kind="Internal").ap()
    rows_dram = nc.dram_tensor("rows_dram", (REGION * E + BLK, ROW), F32, kind="Internal").ap()
    y_dram = nc.dram_tensor("y_dram", (CHOICES * N, C), F32, kind="Internal").ap()
    with ExitStack() as outer:
        carry = outer.enter_context(nc.sbuf_tensor("carry", [P, E], F32))
        table = outer.enter_context(nc.sbuf_tensor("table", [P, 2, NBLK], I32))
        with ExitStack() as ctx:
            attention(nc, ctx, x, xT, ropeT, wqkvT, bqk, bv_rows, wpT, bp_rows, wr, br_rows, x1_dram, rows_dram,
                      carry, table)
        with ExitStack() as ctx:
            experts(nc, ctx, x1_dram, rows_dram, y_dram, table, w_all, out)


def rope_rows():
    import numpy as np

    theta = (np.float32(1.0) / np.float32(10000.0) ** (
        np.float32(2.0) * np.arange(0, HD // 2, dtype=np.float32) / np.float32(HD))).astype(np.float32)
    ang = np.arange(1, T + 1, dtype=np.float32)[None, :] * theta[:, None]
    f = (np.cos(ang) + np.sin(ang)).astype(np.float32)
    f = np.concatenate([f, f], axis=0)
    return np.tile(np.repeat(f, HQ, axis=0), (QUADS, 1))


def kernel(**inputs):
    import numpy as np
    import concourse.bacc as bacc
    from concourse.bass_utils import run_bass_kernel_spmd

    a = {k: np.asarray(v) for k, v in inputs.items()}
    x = a["L0_attn_x"].reshape(N, C)

    def by_channel(w):
        return w.reshape(QUADS, HQ, HD, -1).transpose(0, 2, 1, 3).reshape(C, -1)

    wq, wk, wv = a["L0_attn_W_attn"].reshape(3, C, C)
    bq, bk, bv = a["L0_attn_b_attn"].reshape(3, C)
    arrays = {
        "x": x,
        "xT": x.T,
        "ropeT": rope_rows(),
        "wqkvT": np.concatenate([by_channel(wq), by_channel(wk), wv]).T,
        "bqk": np.concatenate([by_channel(bq), by_channel(bk)], axis=1),
        "bv_rows": np.broadcast_to(bv, (P, C)),
        "wpT": a["L0_attn_W_proj"].T,
        "bp_rows": np.broadcast_to(a["L0_attn_b_proj"], (P, C)),
        "wr": a["L0_ffn_Wr"],
        "br_rows": np.broadcast_to(a["L0_ffn_br"], (P, E)),
        "w_all": np.concatenate([
            a["L0_ffn_W1"],
            a["L0_ffn_W2"].reshape(E, HC, P, C).transpose(0, 2, 1, 3).reshape(E, P, HC * C),
            a["L0_ffn_b1"].reshape(E, HC, P).transpose(0, 2, 1),
            np.broadcast_to(a["L0_ffn_b2"][:, None, :], (E, P, C)),
        ], axis=2).reshape(E * P, WROW),
    }
    arrays = {k: np.ascontiguousarray(v) for k, v in arrays.items()}
    nc = bacc.Bacc("TRN2", target_bir_lowering=False, num_devices=1)
    args = [nc.dram_tensor(f"in_{k}", v.shape, F32, kind="ExternalInput").ap() for k, v in arrays.items()]
    out = nc.dram_tensor("out_0", (N, C), F32, kind="ExternalOutput").ap()
    program(nc, *args, out)
    r = run_bass_kernel_spmd(nc, [{f"in_{k}": v for k, v in arrays.items()}], core_ids=[0])
    return r.results[0]["out_0"].reshape(B, T, C)
```
